# Optimizing a Trainium2 kernel written in Bass

```python
import numpy as np
import jax
import jax.numpy as jnp

def _softmax(x, axis=-1):
    return jax.nn.softmax(x, axis=axis)

def _gelu(x):
    return jax.nn.gelu(x, approximate=True)

def _silu(x):
    return jax.nn.silu(x)

def _sigmoid(x):
    return jax.nn.sigmoid(x)

def _layernorm(x, axis=-1, eps=1e-05):
    m = jnp.mean(x, axis=axis, keepdims=True)
    v = jnp.var(x, axis=axis, keepdims=True)
    return (x - m) / jnp.sqrt(v + eps)

def _scatter_add(tgt, idx, src, axis=0):
    return tgt.at[idx].add(src)

def _segment_sum(src, seg, n):
    return jax.ops.segment_sum(src, seg, n)
kernel_name = 'mk_gnn_resnorm_d1_gnn_r8_0426aa'

def setup_inputs(seed: int=0):
    np.random.seed(seed)
    _w = jnp.asarray

    def _rec_inputs():
        import jax
        import jax.numpy as jnp
        _gk = jax.random.key(seed)
        x = -0.0009044 + 1 * jax.random.normal(jax.random.fold_in(_gk, 1), (12500, 64), jnp.float32)
        src = jax.random.randint(jax.random.fold_in(_gk, 2), (200000,), 0, 12500, jnp.int32)
        dst = jnp.minimum((12500 * jax.random.uniform(jax.random.fold_in(_gk, 3), (200000,)) ** 2.0).astype(jnp.int32), 99999)
        _o = jnp.argsort(dst, stable=True)
        src = src[_o]
        dst = dst[_o]
        edge_attr_64 = 0.000189758 + 1.00013 * jax.random.normal(jax.random.fold_in(_gk, 11), (200000, 64), jnp.float32)
        edge_weight1 = jax.random.uniform(jax.random.fold_in(_gk, 13), (200000, 1), jnp.float32, 0.0, 4.99999)
        return (x, src, dst, edge_attr_64, edge_weight1)
    x, src, dst, edge_attr_64, edge_weight1 = _rec_inputs()

    def _L0_gnn_setup():
        import jax, jax.numpy as jnp
        import numpy as np
        N_NODES = 3125
        N_EDGES = 100000
        NODE = 64
        EDGE = 64
        CUTOFF = 5.0

        def ssp(x):
            return jax.nn.softplus(x) - jnp.log(2.0)
        key = jax.random.key(seed)
        ks = jax.random.split(key, 12)
        s = 0.1
        return {'node_state': jax.random.normal(ks[0], (N_NODES, NODE), dtype=jnp.float32), 'edges': jax.random.randint(ks[1], (N_EDGES, 2), 0, N_NODES, dtype=jnp.int64 if jax.config.jax_enable_x64 else jnp.int32), 'edge_state': jax.random.normal(ks[2], (N_EDGES, EDGE), dtype=jnp.float32), 'edges_distance': jax.random.uniform(ks[3], (N_EDGES, 1), dtype=jnp.float32) * CUTOFF, 'We1': jax.random.normal(ks[4], (EDGE, NODE), dtype=jnp.float32) * s, 'be1': jnp.zeros((NODE,), dtype=jnp.float32), 'We2': jax.random.normal(ks[5], (NODE, NODE), dtype=jnp.float32) * s, 'be2': jnp.zeros((NODE,), dtype=jnp.float32), 'Wn1': jax.random.normal(ks[6], (2 * NODE, 2 * NODE), dtype=jnp.float32) * s, 'bn1': jnp.zeros((2 * NODE,), dtype=jnp.float32), 'Wn2': jax.random.normal(ks[7], (2 * NODE, NODE), dtype=jnp.float32) * s, 'bn2': jnp.zeros((NODE,), dtype=jnp.float32), 'Ws1': jax.random.normal(ks[8], (NODE, NODE), dtype=jnp.float32) * s, 'bs1': jnp.zeros((NODE,), dtype=jnp.float32), 'Ws2': jax.random.normal(ks[9], (NODE, NODE), dtype=jnp.float32) * s, 'bs2': jnp.zeros((NODE,), dtype=jnp.float32)}
    _L0_gnn_all = _L0_gnn_setup()
    _L0_gnn_in = {k: v for k, v in _L0_gnn_all.items() if k in ('We1', 'be1', 'We2', 'be2', 'Wn1', 'bn1', 'Wn2', 'bn2', 'Ws1', 'bs1', 'Ws2', 'bs2')}
    del _L0_gnn_all
    return {'x': x, 'src': src, 'dst': dst, 'edge_attr_64': edge_attr_64, 'edge_weight1': edge_weight1, 'L0_gnn_We1': _L0_gnn_in['We1'], 'L0_gnn_be1': _L0_gnn_in['be1'], 'L0_gnn_We2': _L0_gnn_in['We2'], 'L0_gnn_be2': _L0_gnn_in['be2'], 'L0_gnn_Wn1': _L0_gnn_in['Wn1'], 'L0_gnn_bn1': _L0_gnn_in['bn1'], 'L0_gnn_Wn2': _L0_gnn_in['Wn2'], 'L0_gnn_bn2': _L0_gnn_in['bn2'], 'L0_gnn_Ws1': _L0_gnn_in['Ws1'], 'L0_gnn_bs1': _L0_gnn_in['bs1'], 'L0_gnn_Ws2': _L0_gnn_in['Ws2'], 'L0_gnn_bs2': _L0_gnn_in['bs2']}

def reference(x, src, dst, edge_attr_64, edge_weight1, L0_gnn_We1, L0_gnn_be1, L0_gnn_We2, L0_gnn_be2, L0_gnn_Wn1, L0_gnn_bn1, L0_gnn_Wn2, L0_gnn_bn2, L0_gnn_Ws1, L0_gnn_bs1, L0_gnn_Ws2, L0_gnn_bs2):
    import jax
    import jax.numpy as jnp

    def _L0_gnn_ref(node_state, edges, edge_state, edges_distance, We1, be1, We2, be2, Wn1, bn1, Wn2, bn2, Ws1, bs1, Ws2, bs2):
        import jax, jax.numpy as jnp
        import numpy as np
        N_NODES = 3125
        N_EDGES = 100000
        NODE = 64
        EDGE = 64
        CUTOFF = 5.0

        def ssp(x):
            return jax.nn.softplus(x) - jnp.log(2.0)
        num_edges = edges.shape[0]
        nodes = node_state[edges].reshape(num_edges, -1)
        gates = ssp(edge_state @ We1 + be1) @ We2 + be2
        soft_cutoff = 1.0 - jax.nn.sigmoid(5.0 * (edges_distance - (CUTOFF - 1.5)))
        gates = gates * soft_cutoff
        h = ssp(nodes @ Wn1 + bn1) @ Wn2 + bn2
        messages = h * gates
        message_sum = jnp.zeros_like(node_state).at[edges[:, 1]].add(messages)
        new_state = node_state + (ssp(message_sum @ Ws1 + bs1) @ Ws2 + bs2)
        return new_state
    edge_index_t = jnp.stack([src, dst], axis=1)
    x = _layernorm(x + _L0_gnn_ref(x, edge_index_t, edge_attr_64, edge_weight1, L0_gnn_We1, L0_gnn_be1, L0_gnn_We2, L0_gnn_be2, L0_gnn_Wn1, L0_gnn_bn1, L0_gnn_Wn2, L0_gnn_bn2, L0_gnn_Ws1, L0_gnn_bs1, L0_gnn_Ws2, L0_gnn_bs2), axis=-1)
    return x

_drawn_inputs = setup_inputs


def setup_inputs(seed=0):
    import zlib

    import numpy as np

    out = dict(_drawn_inputs(seed))
    spreads = {'L0_gnn_be1': (0.0, 0.1),
     'L0_gnn_be2': (0.0, 0.1),
     'L0_gnn_bn1': (0.0, 0.402),
     'L0_gnn_bn2': (0.0, 0.1),
     'L0_gnn_bs1': (0.0, 0.367),
     'L0_gnn_bs2': (0.0, 0.1)}
    factors = {}
    for name, (base, spread) in spreads.items():
        noise = np.random.default_rng([zlib.crc32(name.encode()), seed]).standard_normal(out[name].shape)
        drawn = base * np.exp(spread * noise) if base else spread * noise
        out[name] = jnp.asarray(drawn.astype(out[name].dtype))
    for name, factor in factors.items():
        out[name] = (out[name] * factor).astype(out[name].dtype)
    return out
```

```python
from contextlib import ExitStack

import numpy as np
import concourse.bass as bass
from concourse import mybir
from concourse.alu_op_type import AluOpType as ALU

F32 = mybir.dt.float32
BF16 = mybir.dt.bfloat16
I32 = mybir.dt.int32
ACT = mybir.ActivationFunctionType
AX_X = mybir.AxisListType.X
LN2 = float(np.log(2.0))

P = 128
PAIR = 2 * P
QUAD = 2 * PAIR
W = 64
RING = 4
IRING = 4
CLAMP = 1e17
ZMAX = 40.0
EPS = 1e-5


def reached(i, n):
    return not isinstance(i, int) or i >= n


def steps(eng, first, last, peel, unroll, body, tail=0):
    start = first + peel
    assert start % unroll == 0
    stop = start + max(0, (last - tail - start) // unroll * unroll)
    for i in range(first, min(start, last)):
        body(i, i % unroll)
    if stop > start:
        with eng.Fori(start, stop - unroll + 1, unroll) as base:
            for u in range(unroll):
                body(base + u, u)
    for i in range(stop, last):
        body(i, i % unroll)


def per_ring(i, u, ring, count):
    if isinstance(i, int):
        return count * (i // ring + 1)
    return (i - u + ring) * (count // ring)


def gnn_layer(nc, x, src, dst, edge_attr, dist, We1, be1, We2, be2, Wn1, bn1, Wn2, bn2,
              Ws1, bs1, Ws2, bs2, out):
    N, D = x.shape
    E = src.shape[0]
    F = 2 * D
    assert D == 64 and F == P and N > W

    PB = 125
    NB = N // PB
    assert PB * NB == N and NB % 4 == 0
    NG = NB // 4
    SB = -(-N // P)
    SB += SB % 2
    NQ = -(-E // QUAD)
    NPAIR = 2 * NQ
    FULL = E // PAIR
    REM = E - FULL * PAIR
    assert FULL == NPAIR - 1 and REM > 0 and PAIR % REM == 0 and REM % 64 == 0
    NT = 2 * NPAIR
    RG = -(-NPAIR // P)
    RL = NPAIR - (RG - 1) * P

    with ExitStack() as ctx:
        ctx.enter_context(nc.allow_non_contiguous_dma(reason="small tables"))

        def sb(name, shape, dt=F32):
            return ctx.enter_context(nc.sbuf_tensor(name, shape, dt))

        def sem(name):
            return ctx.enter_context(nc.semaphore(name))

        a_tab = nc.dram_tensor("a_tab", (N, F), F32, kind="Internal").ap()
        b_tab = nc.dram_tensor("b_tab", (N, 4 * F), BF16, kind="Internal").ap()
        w_tab = nc.dram_tensor("w_tab", (1, RG * P), I32, kind="Internal").ap()

        ident = sb("ident", [P, P])
        identb = sb("identb", [P, P], BF16)
        iota_i = sb("iota_i", [P, P], I32)
        iota_w = sb("iota_w", [P, P])
        iota_n = sb("iota_n", [P, P])
        ones_b = sb("ones_b", [P, P], BF16)
        we1 = sb("we1", [P, P])
        we2 = sb("we2", [P, P])
        wn1 = sb("wn1", [P, 2, F])
        wn2 = sb("wn2", [P, D])
        ws1 = sb("ws1", [P, D])
        ws2 = sb("ws2", [P, D])
        ws2m = sb("ws2m", [P, 1])
        be1c = sb("be1c", [P, 1])
        be1l = sb("be1l", [P, 1])
        bs1c = sb("bs1c", [P, 1])
        bs1l = sb("bs1l", [P, 1])
        bn1r = sb("bn1r", [P, F])
        bs2r = sb("bs2r", [P, D])
        brow = sb("brow", [P, 2, 4, D])
        brow1 = sb("brow1", [P, QUAD], BF16)
        brow2 = sb("brow2", [P, QUAD], BF16)
        biasb = sb("biasb", [P, QUAD], BF16)
        cexp = sb("cexp", [P, 1])
        epsc = sb("epsc", [P, 1])
        halfc = sb("halfc", [P, 1])

        acc = sb("acc", [P, SB * P])
        RI, RF = 2 * RG * PAIR, 3 * RG * PAIR
        assert RI + RF <= SB * P
        rows_i = acc[:, 0:RI].bitcast(I32).rearrange("p (k g e) -> p k g e", k=2, e=PAIR)
        rows_f = acc[:, RI:RI + RF].rearrange("p (k g e) -> p k g e", k=3, e=PAIR)
        dmin = sb("dmin", [P, RG])
        w_i = sb("w_i", [P, RG], I32)
        w_all = sb("w_all", [P, NPAIR], I32)
        srcT = sb("srcT", [P, NT], I32)
        dstT = sb("dstT", [P, NT])
        relT = sb("relT", [P, NT])
        cutT = sb("cutT", [P, NT])
        relmax = sb("relmax", [P, 1])
        flagf = sb("flagf", [1, 2])
        flag_i = sb("flag_i", [1, 2], I32)

        xs = sb("xs", [P, NB, D])
        xmean = sb("xmean", [P, NB])
        stage_a = sb("stage_a", [P, 2, 4, F])
        stage_b = sb("stage_b", [P, 2, 4, 4 * F], BF16)
        rest_b = sb("rest_b", [P, 2, 4, F])

        idxb = sb("idxb", [P, IRING, 8], I32)
        ea = sb("ea", [P, RING, 2, P])
        ga = sb("ga", [P, RING, 4, F])
        bw = sb("bw", [P, RING, 2, 2, F], BF16)
        oh = sb("oh", [P, RING, 4, P])
        eaT = sb("eaT", [P, 2, PAIR])
        ohT = sb("ohT", [P, 2, QUAD], BF16)
        hid = sb("hid", [P, 2, QUAD + PAIR])
        gcut = sb("gcut", [P, PAIR])
        msg = sb("msg", [P, 2, 4, D])

        late_words = 2 * 2 * (QUAD + PAIR) + 8 + 8 + 2 * 4 * P + 4 * 4 * F // 2
        shared = sb("shared", [P, max(NB // 2 * PB, late_words)])
        xT = shared[:, 0:NB // 2 * PB].rearrange("p (k c) -> p k c", c=PB)
        taken = [0]

        def late(shape, dt=F32):
            words = int(np.prod(shape)) // (2 if dt == BF16 else 1)
            part = shared[:, taken[0]:taken[0] + words]
            taken[0] += words
            if dt != F32:
                part = part.bitcast(dt)
            names = "abc"[:len(shape)]
            return part.rearrange(f"p ({' '.join(names)}) -> p {' '.join(names)}", **dict(zip(names, shape)))

        ex = late([2, QUAD + PAIR])
        lg = late([2, QUAD + PAIR])
        gen_idx = late([8], I32)
        gen_rel = late([2, 4])
        gen_oh = late([2, 4, P])
        gen_b = late([4, 4 * F], BF16)
        assert taken[0] <= late_words

        dd = sb("dd", [P, 4, 4, D])
        sq = sb("sq", [P, 2, 4, D])
        ssum = sb("ssum", [P, 2, 4])
        lvar = sb("lvar", [P, 2, 4])
        rstd = sb("rstd", [P, 2, 4])
        outs = sb("outs", [P, 2, 4, D])

        ps = ctx.enter_context(nc.psum_tensor("ps", [P, 8, 512], F32))
        ps_eaT, ps_ohT, ps_hg, ps_s = ps[:, 4, :], ps[:, 5, :], ps[:, 6, :], ps[:, 7, :]

        ld_src, ld_dst, ld_dist, ld_x, ld_w, ld_bd = (sem(n) for n in (
            "ld_src", "ld_dst", "ld_dist", "ld_x", "ld_w", "ld_bd"))
        zeroed, consts, iotas, dve_chain, act_chain = (sem(n) for n in (
            "zeroed", "consts", "iotas", "dve_chain", "act_chain"))
        rows_ready = [sem(f"rows_ready{k}") for k in range(2)]
        row_t, row_dve, row_act = sem("row_t"), sem("row_dve"), sem("row_act")
        acc_zeroed = sem("acc_zeroed")
        w_ready, w_stored, w_loaded = sem("w_ready"), sem("w_stored"), sem("w_loaded")
        relm_ready, relm_t, flag_ready = sem("relm_ready"), sem("relm_t"), sem("flag_ready")
        cut_exp = sem("cut_exp")
        xT_t, xT_e = sem("xT_t"), sem("xT_e")
        tab_mm, tab_ready = sem("tab_mm"), sem("tab_ready")
        b1_ready, rest_ready, b2_ready = sem("b1_ready"), sem("rest_ready"), sem("b2_ready")
        a_stored = [sem(f"a_stored{k}") for k in range(2)]
        b_stored = [sem(f"b_stored{k}") for k in range(2)]
        quads_begun = sem("quads_begun")
        s_idx = [sem(f"s_idx{k}") for k in range(IRING)]
        s_ea = [sem(f"s_ea{k}") for k in range(RING)]
        s_ga = [sem(f"s_ga{k}") for k in range(RING)]
        s_bw = [sem(f"s_bw{k}") for k in range(RING)]
        ea_t, ea_e, oh_b, oh_t, oh_e, z_mm, z_exp, z_clamp, z_ln, hid_b, hg_mm, gc_b, msg_b, sc_mm, flushed = (
            sem(n) for n in ("ea_t", "ea_e", "oh_b", "oh_t", "oh_e", "z_mm", "z_exp", "z_clamp", "z_ln",
                             "hid_b", "hg_mm", "gc_b", "msg_b", "sc_mm", "flushed"))
        g_idx, g_b = sem("g_idx"), sem("g_b")
        g_rel = sem("g_rel")
        g_oh = [sem(f"g_oh{k}") for k in range(2)]
        g_mm = [sem(f"g_mm{k}") for k in range(2)]
        g_add = [sem(f"g_add{k}") for k in range(2)]
        n_mm, n_exp, n_clamp, n_ln, n_hid, y_mm, y_add, y_sq, y_sum, y_lv, y_rstd, y_out = (
            sem(n) for n in ("n_mm", "n_exp", "n_clamp", "n_ln", "n_hid", "y_mm", "y_add", "y_sq", "y_sum",
                             "y_lv", "y_rstd", "y_out"))
        xc_ready = sem("xc_ready")
        s_out = [sem(f"s_out{k}") for k in range(2)]

        block = ctx.enter_context(nc.Block())

        N_LD_W = 13
        N_LD_ROWS = (RG > 1) + 1 + PAIR // REM
        a_uses = [-(-(NG - k) // 2) for k in range(2)]

        def row_views(t):
            full = t[0:FULL * PAIR].rearrange("(r e) -> r e", e=PAIR)
            head = None
            if RG > 1:
                head = full[0:(RG - 1) * P, :].rearrange("(g p) e -> p g e", p=P)
            return head, full[(RG - 1) * P:FULL, :], t[FULL * PAIR:E].rearrange("(r e) -> r e", r=1)

        def quad_cols(i, size, scale):
            return bass.ds(i * scale, size)

        def general_of(eng):
            eng.wait_ge(flag_ready, 1)
            return eng.value_load(flag_i[0:1, 0:1], min_val=0, max_val=1)

        @block.sync
        def _(sp):
            def load_rows(t, to, done):
                head, tail, rest = row_views(t)
                if head is not None:
                    sp.dma_start(to[:, 0:RG - 1, :], head).then_inc(done, 16)
                sp.dma_start(to[0:RL - 1, RG - 1, :], tail).then_inc(done, 16)
                for k in range(PAIR // REM):
                    sp.dma_start(to[RL - 1:RL, RG - 1, k * REM:(k + 1) * REM], rest).then_inc(done, 16)

            load_rows(src, rows_i[:, 0], ld_src)
            sp.dma_start(xs[0:PB, :, :], x.rearrange("(p b) d -> p b d", b=NB)).then_inc(ld_x, 16)
            sp.dma_start(wn1[0:D, :, :], Wn1.rearrange("(h k) f -> k h f", h=2)).then_inc(ld_w, 16)
            sp.dma_start(wn1[D:P, :, :], Wn1.rearrange("(h k) f -> k h f", h=2)).then_inc(ld_w, 16)
            sp.dma_start(bn1r[:, :], bn1.rearrange("(a f) -> a f", a=1).broadcast_to([P, F])).then_inc(ld_w, 16)
            load_rows(dst, rows_i[:, 1], ld_dst)
            load_rows(dist.rearrange("e a -> (e a)"), rows_f[:, 2], ld_dist)
            col = lambda v: v.rearrange("(f a) -> f a", a=1)
            row = lambda v: v.rearrange("(a f) -> a f", a=1)
            for h in range(2):
                half = slice(h * D, (h + 1) * D)
                sp.dma_start(be1c[half, :], col(be1)).then_inc(ld_w, 16)
                sp.dma_start(bs1c[half, :], col(bs1)).then_inc(ld_w, 16)
                sp.dma_start(ws1[half, :], Ws1).then_inc(ld_w, 16)
                sp.dma_start(ws2[half, :], Ws2).then_inc(ld_w, 16)
            sp.dma_start(bs2r[:, :], row(bs2).broadcast_to([P, D])).then_inc(ld_w, 16)
            sp.dma_start(wn2[:, :], Wn2).then_inc(ld_w, 16)
            sp.wait_ge(zeroed, 1)
            for h in range(2):
                half = slice(h * D, (h + 1) * D)
                sp.dma_start(we1[half, half], We1).then_inc(ld_bd, 16)
                sp.dma_start(we2[half, half], We2).then_inc(ld_bd, 16)
            for r in (0, 32, 64):
                for h, v in enumerate((bn2, be2)):
                    for k in range(4):
                        sp.dma_start(brow[r:r + 1, h, k, :], row(v)).then_inc(ld_bd, 16)

            sp.wait_ge(w_ready, 1)
            wv = w_tab.rearrange("a (g p) -> p (a g)", p=P)
            if RG > 1:
                sp.dma_start(wv[:, 0:RG - 1], w_i[:, 0:RG - 1]).then_inc(w_stored, 16)
            sp.dma_start(wv[0:RL, RG - 1:RG], w_i[0:RL, RG - 1:RG]).then_inc(w_stored, 16)
            sp.wait_ge(w_stored, 16 * (1 + (RG > 1)))
            sp.dma_start(w_all[:, :], w_tab[:, 0:NPAIR].broadcast_to([P, NPAIR])).then_inc(w_loaded, 16)

            av = a_tab.rearrange("(p b) f -> p b f", b=NB)
            bv = b_tab.rearrange("(p b) f -> p b f", b=NB)

            def store_a(g, u):
                sp.wait_ge(tab_ready, g + 1)
                sp.dma_start(av[:, bass.ds(g * 4, 4), :], stage_a[0:PB, u, :, :]).then_inc(a_stored[u], 16)

            def store_b(g, u):
                sp.wait_ge(tab_ready, g + (NG + 1))
                sp.dma_start(bv[:, bass.ds(g * 4, 4), :], stage_b[0:PB, u, :, :]).then_inc(b_stored[u], 16)

            steps(sp, 0, NG, 2, 2, store_a)
            steps(sp, 0, NG, 2, 2, store_b)

            def load_ea(q, u):
                if reached(q, RING):
                    sp.wait_ge(ea_t, q - (RING - 1))
                if isinstance(q, int) and q == NQ - 1:
                    full = edge_attr[q * QUAD:q * QUAD + PAIR, :].rearrange("(p j) d -> p (j d)", j=2)
                    sp.dma_start(ea[:, u, 0, :], full).then_inc(s_ea[u], 8 * 2)
                    part = edge_attr[FULL * PAIR:E, :].rearrange("(p j) d -> p (j d)", j=2)
                    sp.dma_start(ea[0:REM // 2, u, 1, :], part).then_inc(s_ea[u], 16)
                else:
                    rows = edge_attr[bass.ds(q * QUAD, QUAD), :]
                    sp.dma_start(ea[:, u, :, :], rows.rearrange("(k p j) d -> p k (j d)", p=P, j=2)).then_inc(s_ea[u], 16)

            def load_idx(q, slot):
                if reached(q, 2 * IRING):
                    sp.wait_ge(z_mm, q - (2 * IRING - 2))
                n = 8 if not isinstance(q, int) or q + 1 < NQ else 4
                sp.dma_start(idxb[:, slot, 0:n], srcT[:, quad_cols(q, n, 4)]).then_inc(s_idx[slot], 16)

            firsts = [None] * 4

            def fast_step(q, v):
                u = v % RING
                if isinstance(q, int) and q == 0:
                    load_idx(0, 0)
                if v % 2 == 0:
                    if not isinstance(q, int) or q + 2 < NQ:
                        load_idx(q + 2, (v // 2 + 1) % IRING)
                    if isinstance(q, int) and q + 1 == NQ:
                        firsts[0:2] = [sp.value_load(w_all[0:1, q * 2 + k:q * 2 + k + 1], min_val=0, max_val=N - W)
                                       for k in range(2)]
                    else:
                        _, firsts[:] = nc.values_load_multi_w_load_instructions(
                            w_all[0:1, bass.ds(q * 2, 4)], engines=(mybir.EngineType.SP,), min_val=0, max_val=N - W)
                load_ea(q, u)
                if reached(q, RING):
                    sp.wait_ge(z_mm, q - (RING - 1))
                for k in range(2):
                    rows = b_tab[bass.ds(firsts[2 * (v % 2) + k], W), :].rearrange("w (h cf) -> h w cf", h=2)
                    sp.dma_start(bw[:, u, k, :, :].rearrange("p c f -> p (c f)"), rows).then_inc(s_bw[u], 16)

            def general_step(q, u):
                if reached(q, 1):
                    sp.wait_ge(s_ga[0], q * 64)
                if reached(q, 1):
                    sp.wait_ge(g_b, q * 64)
                sp.dma_start(gen_idx[:, 0:4], srcT[:, quad_cols(q, 4, 4)]).then_inc(g_idx, 16)
                sp.dma_start(gen_idx[:, 4:8], gen_dst[:, quad_cols(q, 4, 4)]).then_inc(g_idx, 16)
                load_ea(q, u)

            gen_dst = relT[:, :].bitcast(I32)
            general = general_of(sp)
            for k in range(2):
                sp.wait_ge(b_stored[k], 16 * a_uses[k])
            with sp.If(general):
                sp.wait_ge(g_rel, 1)
                steps(sp, 0, NQ, RING, RING, general_step, tail=1)
            with sp.Else():
                steps(sp, 0, NQ, 2 * IRING, 2 * IRING, fast_step, tail=4)

            ov = out.rearrange("(p b) d -> p b d", b=NB)

            def store_out(k, u):
                sp.wait_ge(y_out, k + 1)
                sp.dma_start(ov[:, bass.ds(k * 4, 4), :], outs[0:PB, u, :, :]).then_inc(s_out[u], 16)

            steps(sp, 0, NG, 2, 2, store_out)
            for k in range(2):
                sp.wait_ge(s_out[k], 16 * a_uses[k])

        @block.gpsimd
        def _(pool):
            pool.memset(ident[:, :], 0.0).then_inc(consts, 1)
            pool.wait_ge(consts, 1)
            pool.affine_select(out=ident[:, :], in_=ident[:, :], compare_op=ALU.not_equal, fill=1.0,
                               base=0, pattern=[[-1, P]], channel_multiplier=1).then_inc(consts, 1)
            pool.iota(iota_i[:, :], pattern=[[1, P]], base=0, channel_multiplier=0).then_inc(iotas, 1)

            pool.wait_ge(row_t, 3 * RG)
            pool.wait_ge(w_ready, 1)
            pool.memset(acc[:, :], 0.0).then_inc(acc_zeroed, 1)

            def gather_rows(to, table, idx, done):
                pool.sem_inc(quads_begun, 1)
                for t in range(4):
                    pool.indirect_dma_start(to[:, t, :], None, table,
                                            bass.IndirectOffsetOnAxis(ap=idx[:, t:t + 1], axis=0)).then_inc(done, 16)

            def fast_step(q, v):
                u = v % RING
                pool.wait_ge(s_idx[v // 2], per_ring(q, v, 2 * IRING, 16))
                if reached(q, RING):
                    pool.wait_ge(z_mm, q - (RING - 1))
                gather_rows(ga[:, u], a_tab, idxb[:, v // 2, 4 * (v % 2):4 * (v % 2) + 4], s_ga[u])

            def general_step(q, u):
                pool.wait_ge(g_idx, q * 32 + 32)
                if reached(q, 1):
                    pool.wait_ge(z_mm, q)
                gather_rows(ga[:, 0], a_tab, gen_idx[:, 0:4], s_ga[0])
                gather_rows(gen_b, b_tab, gen_idx[:, 4:8], g_b)

            general = general_of(pool)
            for k in range(2):
                pool.wait_ge(a_stored[k], 16 * a_uses[k])
            with pool.If(general):
                for k in range(2):
                    pool.wait_ge(b_stored[k], 16 * a_uses[k])
                steps(pool, 0, NQ, RING, RING, general_step, tail=1)
            with pool.Else():
                steps(pool, 0, NQ, 2 * IRING, 2 * IRING, fast_step)

        @block.tensor
        def _(pe):
            pe.wait_ge(consts, 2)
            for k in range(3):
                if k < 2:
                    pe.wait_ge(rows_ready[k], 1)
                else:
                    pe.wait_ge(ld_dist, 16 * N_LD_ROWS)
                for g in range(RG):
                    n = k * RG + g
                    rows = P if g < RG - 1 else RL
                    if n >= 2:
                        if n - 2 < RG:
                            pe.wait_ge(row_dve, n - 1)
                        else:
                            pe.wait_ge(row_act, n - 1 - RG)
                    for j in range(2):
                        mm = pe.transpose(ps[:, n % 2, j * P:j * P + rows],
                                          rows_f[0:rows, k, g, j:PAIR:2], ident[0:rows, 0:rows])
                    mm.then_inc(row_t, 1)
            pe.wait_ge(row_act, 2 * RG)

            pe.wait_ge(ld_x, 16)
            pe.wait_ge(ld_w, 16 * N_LD_W)

            def transpose_x(g, u):
                if reached(g, 2):
                    pe.wait_ge(xT_e, g - 1)
                for k in range(2):
                    blocks = xs[0:PB, bass.ds(g * 4 + 2 * k, 2), :].rearrange("p b d -> p (b d)")
                    mm = pe.transpose(ps[:, 4 + u, k * PB:(k + 1) * PB], blocks, ident[0:PB, 0:PB])
                mm.then_inc(xT_t, 1)

            def table_mm(half, base):
                def body(g, u):
                    pe.wait_ge(xT_e, g + 1)
                    if base or g >= 2:
                        pe.wait_ge(tab_ready, max(base, g + base - 1))
                    for par in range(2):
                        rows = slice(par * D, (par + 1) * D)
                        for k in range(2):
                            mm = pe.matmul(ps[0:PB, 2 * u + par, k * F:(k + 1) * F],
                                           xT[rows, bass.ds(g * 2 + k, 1), :].rearrange("f a p -> f (a p)"),
                                           wn1[rows, half, :], start=True, stop=True)
                    mm.then_inc(tab_mm, 1)
                return body

            mm_a = table_mm(0, 0)

            def both(g, u):
                transpose_x(g, u)
                mm_a(g, u)

            for g in range(NG):
                both(g, g % 2)
            mm_b = table_mm(1, NG)
            for g in range(NG):
                mm_b(g, g % 2)

            pe.wait_ge(relm_ready, 1)
            pe.wait_ge(tab_ready, 2 * NG)
            pe.transpose(ps[0:1, 0, 0:P], relmax[:, 0:1], ident[:, :]).then_inc(relm_t, 1)
            pe.wait_ge(ld_bd, 16)

            def transpose_ea(q, u):
                pe.wait_ge(s_ea[u], per_ring(q, u, RING, 16) + (16 if isinstance(q, int) and q == NQ - 1 else 0))
                if reached(q, 1):
                    pe.wait_ge(ea_e, q)
                for k in range(2):
                    mm = pe.transpose(ps_eaT[:, k * P:(k + 1) * P], ea[:, u, k, :], ident[:, :])
                mm.then_inc(ea_t, 1)

            def source_part(q, u, slot, landed):
                pe.wait_ge(s_ga[slot], landed)
                if reached(q, 2):
                    pe.wait_ge(hid_b, q - 1)
                z = ps[:, 2 * (u % 2), :]
                for t in range(4):
                    pe.matmul(z[:, t * P:(t + 1) * P], ga[:, slot, t, :], ident[:, :], is_transpose=True,
                              start=(t == 0), stop=False, skip_group_check=True)

            def gate_part(q, u):
                pe.wait_ge(ea_e, q + 1)
                pe.matmul(ps[:, 2 * (u % 2) + 1, 0:PAIR], we1[:, :], eaT[:, u % 2, :], start=True, stop=True)

            def transposes(q, u):
                transpose_ea(q, u)
                pe.wait_ge(oh_b, q + 1)
                if reached(q, 1):
                    pe.wait_ge(oh_e, q)
                for t in range(4):
                    mm = pe.transpose(ps_ohT[:, t * P:(t + 1) * P], oh[:, u, t, :], ident[:, :])
                mm.then_inc(oh_t, 1)

            def front(q, u):
                source_part(q, u, u, per_ring(q, u, RING, 64))
                gate_part(q, u)
                pe.wait_ge(oh_e, q + 1)
                pe.wait_ge(s_bw[u], per_ring(q, u, RING, 32))
                z = ps[:, 2 * (u % 2), :]
                for k in range(2):
                    for c in range(2):
                        cols = slice(k * PAIR, (k + 1) * PAIR)
                        mm = pe.matmul(z[:, cols], bw[:, u, k, c, :], ohT[:, u % 2, cols],
                                       start=False, stop=(c == 1), skip_group_check=True)
                mm.then_inc(z_mm, 1)

            def mid(q, u):
                pe.wait_ge(hid_b, q + 1)
                if reached(q, 1):
                    pe.wait_ge(msg_b, q)
                pe.matmul(ps_hg[:, :], ones_b[:, :], biasb[:, :], start=True, stop=False, skip_group_check=True)
                for t in range(4):
                    pe.matmul(ps_hg[:, t * D:(t + 1) * D], hid[:, u % 2, t * P:(t + 1) * P], wn2[:, :],
                              start=False, stop=False, skip_group_check=True)
                for k in range(2):
                    mm = pe.matmul(ps_hg[:, PAIR + k * P:PAIR + (k + 1) * P],
                                   hid[:, u % 2, QUAD + k * P:QUAD + (k + 1) * P], we2[:, :],
                                   start=False, stop=(k == 1), skip_group_check=True)
                mm.then_inc(hg_mm, 1)

            def back(q, u):
                pe.wait_ge(msg_b, q + 1)
                if reached(q, 1):
                    pe.wait_ge(flushed, q)
                for k in range(2):
                    for j in range(2):
                        mm = pe.matmul(ps_s[k * D:(k + 1) * D, 0:W], msg[:, u % 2, 2 * k + j, :],
                                       oh[:, u, 2 * k + j, 0:W], start=(j == 0), stop=(j == 1))
                mm.then_inc(sc_mm, 1)

            def fast_step(s, u):
                known = isinstance(s, int)
                if known and s == 0:
                    transposes(0, 0)
                if not known or s < NQ:
                    front(s, u)
                if not known or s + 1 < NQ:
                    transposes(s + 1, (u + 1) % RING)
                if not known or s >= 2:
                    back(s - 2, (u - 2) % RING)
                if not known or 1 <= s <= NQ:
                    mid(s - 1, (u - 1) % RING)

            def general_step(q, u):
                transpose_ea(q, u)
                source_part(q, u, 0, q * 64 + 64)
                gate_part(q, u)
                pe.wait_ge(g_b, q * 64 + 64)
                z = ps[:, 2 * (u % 2), :]
                for t in range(4):
                    for c in range(3):
                        mm = pe.matmul(z[:, t * P:(t + 1) * P], gen_b[:, t, c * F:(c + 1) * F], identb[:, :],
                                       start=False, stop=(c == 2), skip_group_check=True)
                mm.then_inc(z_mm, 1)
                mid(q, u)
                with pe.Fori(0, SB // 2) as b:
                    for k in range(2):
                        pe.wait_ge(msg_b, q + 1)
                        pe.wait_ge(g_oh[k], q * (SB // 2) + b + 1)
                        pe.wait_ge(g_add[1 - k], q * (SB // 2) + b + 1)
                        for t in range(4):
                            mm = pe.matmul(ps_s[0:D, 0:P], msg[:, u % 2, t, :], gen_oh[:, k, t, :],
                                           start=(t == 0), stop=(t == 3))
                        mm.then_inc(g_mm[k], 1)

            general = general_of(pe)
            with pe.If(general):
                steps(pe, 0, NQ, RING, RING, general_step, tail=1)
            with pe.Else():
                steps(pe, 0, NQ + 2, RING, RING, fast_step, tail=4)

            accv = acc[:, 0:N].rearrange("f (p b) -> f b p", b=NB)

            def node_hidden(k, u):
                if reached(k, 2):
                    pe.wait_ge(n_hid, k - 1)
                for h in range(2):
                    mm = pe.matmul(ps[h * D:(h + 1) * D, u, 0:2 * PB].rearrange("f (b p) -> f b p", b=2),
                                   ws1[:, :], accv[:, bass.ds(k * 4 + 2 * h, 2), :],
                                   start=True, stop=True)
                mm.then_inc(n_mm, 1)

            def node_out(k, u):
                pe.wait_ge(n_hid, k + 1)
                if reached(k, 2):
                    pe.wait_ge(y_add, k - 1)
                for h in range(2):
                    for c in range(2):
                        rows = slice(h * D, (h + 1) * D)
                        mm = pe.matmul(ps[0:PB, 4 + 2 * u + h, c * D:(c + 1) * D],
                                       hid[rows, u, c * PB:(c + 1) * PB], ws2[rows, :], start=True, stop=True)
                mm.then_inc(y_mm, 1)

            def node_step(k, u):
                known = isinstance(k, int)
                if not known or k < NG:
                    node_hidden(k, u)
                if not known or k >= 1:
                    node_out(k - 1, (u - 1) % 2)

            pe.wait_ge(xc_ready, 1)
            pe.wait_ge(flushed, NQ)
            for k in range(NG + 1):
                node_step(k, k % 2)

        @block.scalar
        def _(act):
            act.preload_act_table_set("natural_log_exp_and_others")
            act.wait_ge(iotas, 1)
            act.copy(iota_n[:, :], iota_i[:, :]).then_inc(act_chain, 1)
            act.wait_ge(ld_dst, 16 * N_LD_ROWS)
            if RG > 1:
                act.copy(rows_f[:, 1, 0:RG - 1, :], rows_i[:, 1, 0:RG - 1, :])
            act.copy(rows_f[0:RL, 1, RG - 1, :], rows_i[0:RL, 1, RG - 1, :]).then_inc(rows_ready[1], 1)
            for k, to in ((1, dstT), (2, cutT)):
                for g in range(RG):
                    n = k * RG + g
                    rows = P if g < RG - 1 else RL
                    act.wait_ge(row_t, n + 1)
                    tv = to[:, 2 * P * g:2 * (P * g + rows)].rearrange("p (r j) -> p j r", j=2)
                    pv = ps[:, n % 2, 0:PAIR].rearrange("p (j r) -> p j r", j=2)[:, :, 0:rows]
                    act.copy(tv, pv).then_inc(row_act, 1)
            act.wait_ge(row_act, 2 * RG)
            act.wait_ge(zeroed, 1)
            act.activation(cutT[:, :], cutT[:, :], ACT.Exp, bias=cexp[:, 0:1], scale=5.0).then_inc(cut_exp, 1)

            def evacuate_x(g, u):
                act.wait_ge(xT_t, g + 1)
                act.copy(xT[:, bass.ds(g * 2, 2), :],
                         ps[:, 4 + u, 0:2 * PB].rearrange("p (k c) -> p k c", k=2)).then_inc(xT_e, 1)

            steps(act, 0, NG, 2, 2, evacuate_x)

            def split_b(g, u):
                act.wait_ge(tab_mm, g + (NG + 1))
                if reached(g, 2):
                    act.wait_ge(b_stored[u], per_ring(g, u, 2, 16) - 16)
                act.copy(stage_b[0:PB, u, :, 0:F].rearrange("p (k r) f -> p r k f", r=2),
                         ps[0:PB, 2 * u:2 * u + 2, 0:2 * F].rearrange("p r (k f) -> p r k f", f=F)).then_inc(b1_ready, 1)
                act.wait_ge(rest_ready, g + 1)
                act.copy(stage_b[0:PB, u, :, 2 * F:3 * F], rest_b[0:PB, u, :, :]).then_inc(b2_ready, 1)

            steps(act, 0, NG, 2, 2, split_b)

            def evacuate_ea(q, u):
                act.wait_ge(ea_t, q + 1)
                if reached(q, 2):
                    act.wait_ge(z_mm, q - 1)
                act.copy(eaT[:, u % 2, :], ps_eaT[:, 0:PAIR]).then_inc(ea_e, 1)

            def softplus_exp(q, u):
                act.wait_ge(z_mm, q + 1)
                if reached(q, 2):
                    act.wait_ge(z_ln, q - 1)
                act.activation(ex[:, u % 2, 0:QUAD], ps[:, 2 * (u % 2), :], ACT.Exp)
                act.activation(ex[:, u % 2, QUAD:QUAD + PAIR], ps[:, 2 * (u % 2) + 1, 0:PAIR], ACT.Exp,
                               bias=be1c[:, 0:1]).then_inc(z_exp, 1)

            def softplus_ln(q, u):
                act.wait_ge(z_clamp, q + 1)
                if reached(q, 2):
                    act.wait_ge(hid_b, q - 1)
                act.activation(lg[:, u % 2, :], ex[:, u % 2, :], ACT.Ln, bias=halfc[:, 0:1], scale=0.5).then_inc(z_ln, 1)

            def evacuate(q, u):
                evacuate_ea(q, u)
                act.wait_ge(oh_t, q + 1)
                act.copy(ohT[:, u % 2, :], ps_ohT[:, :]).then_inc(oh_e, 1)

            def fast_step(q, u):
                if isinstance(q, int) and q == 0:
                    evacuate(0, 0)
                softplus_exp(q, u)
                if not isinstance(q, int) or q + 1 < NQ:
                    evacuate(q + 1, (u + 1) % RING)
                softplus_ln(q, u)

            def general_step(q, u):
                evacuate_ea(q, u)
                softplus_exp(q, u)
                softplus_ln(q, u)

            general = general_of(act)
            with act.If(general):
                steps(act, 0, NQ, RING, RING, general_step, tail=1)
            with act.Else():
                steps(act, 0, NQ, RING, RING, fast_step, tail=1)

            def node_softplus(k, u):
                act.wait_ge(n_clamp, k + 1)
                act.activation(ex[:, u, 0:2 * PB], ex[:, u, 0:2 * PB], ACT.Exp).then_inc(n_exp, 1)
                act.wait_ge(n_exp, k + 1)
                if reached(k, 2):
                    act.wait_ge(n_hid, k - 1)
                act.activation(lg[:, u, 0:2 * PB], ex[:, u, 0:2 * PB], ACT.Ln, bias=halfc[:, 0:1],
                               scale=0.5).then_inc(n_ln, 1)

            def node_norm(k, u):
                act.wait_ge(y_add, k + 1)
                if reached(k, 2):
                    act.wait_ge(y_sum, k - 1)
                act.activation(sq[0:PB, u, :, :], dd[0:PB, u, :, :], ACT.Square).then_inc(y_sq, 1)
                act.wait_ge(y_sum, k + 1)
                act.activation(lvar[0:PB, u, :], ssum[0:PB, u, :], ACT.Ln, bias=epsc[0:PB, 0:1],
                               scale=1.0 / D).then_inc(y_lv, 1)
                act.wait_ge(y_lv, k + 1)
                act.activation(rstd[0:PB, u, :], lvar[0:PB, u, :], ACT.Exp, scale=-0.5).then_inc(y_rstd, 1)

            def node_step(k, u):
                known = isinstance(k, int)
                if not known or k < NG:
                    node_softplus(k, u)
                if not known or k >= 1:
                    node_norm(k - 1, (u - 1) % 2)

            steps(act, 0, NG + 1, 2, 2, node_step, tail=1)

        @block.vector
        def _(dve):
            chain = [0]

            def link(ins):
                chain[0] += 1
                ins.then_inc(dve_chain, 1)
                dve.wait_ge(dve_chain, chain[0])

            dve.memset(we1[:, :], 0.0)
            dve.memset(we2[:, :], 0.0)
            dve.memset(brow[:, :, :, :], 0.0)
            dve.memset(biasb[:, :], 0.0)
            dve.memset(ones_b[:, :], 1.0)
            dve.memset(cexp[:, :], -17.5)
            dve.memset(epsc[:, :], EPS)
            dve.memset(halfc[:, :], 0.5)
            dve.memset(stage_b[:, :, :, 3 * F:4 * F], 0.0).then_inc(zeroed, 1)

            dve.wait_ge(ld_src, 16 * N_LD_ROWS)
            if RG > 1:
                dve.tensor_copy(rows_f[:, 0, 0:RG - 1, :], rows_i[:, 0, 0:RG - 1, :])
            dve.tensor_copy(rows_f[0:RL, 0, RG - 1, :], rows_i[0:RL, 0, RG - 1, :]).then_inc(rows_ready[0], 1)
            for g in range(RG):
                rows = P if g < RG - 1 else RL
                dve.wait_ge(row_t, g + 1)
                tv = srcT[:, 2 * P * g:2 * (P * g + rows)].rearrange("p (r j) -> p j r", j=2)
                pv = ps[:, g % 2, 0:PAIR].rearrange("p (j r) -> p j r", j=2)[:, :, 0:rows]
                dve.tensor_copy(tv, pv).then_inc(row_dve, 1)

            dve.wait_ge(rows_ready[1], 1)
            if RG > 1:
                dve.tensor_reduce(dmin[:, 0:RG - 1], rows_f[:, 1, 0:RG - 1, :], AX_X, ALU.min)
            link(dve.tensor_reduce(dmin[0:RL, RG - 1:RG], rows_f[0:RL, 1, RG - 1, :], AX_X, ALU.min))
            if RG > 1:
                dve.tensor_scalar(w_i[:, 0:RG - 1], dmin[:, 0:RG - 1], float(N - W), None, ALU.min)
            dve.tensor_scalar(w_i[0:RL, RG - 1:RG], dmin[0:RL, RG - 1:RG], float(N - W), None, ALU.min).then_inc(w_ready, 1)

            def table_a(g, u):
                dve.wait_ge(tab_mm, g + 1)
                if reached(g, 2):
                    dve.wait_ge(a_stored[u], per_ring(g, u, 2, 16) - 16)
                for r in range(2):
                    ins = dve.tensor_tensor(stage_a[0:PB, u, r:4:2, :],
                                            ps[0:PB, 2 * u + r, 0:2 * F].rearrange("p (k f) -> p k f", f=F),
                                            bn1r[0:PB, :].unsqueeze(1).broadcast_to([PB, 2, F]), ALU.add)
                ins.then_inc(tab_ready, 1)

            dve.wait_ge(ld_w, 16 * N_LD_W)
            steps(dve, 0, NG, 2, 2, table_a)

            dve.wait_ge(ld_bd, 16 * 28)
            bflat = brow[:, :, :, :].rearrange("p h k d -> p (h k d)")
            dve.tensor_scalar(be1l[:, :], be1c[:, :], LN2, None, ALU.subtract)
            dve.tensor_scalar(bs1l[:, :], bs1c[:, :], LN2, None, ALU.subtract)
            link(dve.tensor_copy(brow1[:, :], bflat))
            link(dve.tensor_tensor(bflat, bflat, brow1[:, :], ALU.subtract))
            link(dve.tensor_copy(brow2[:, :], bflat))
            link(dve.tensor_tensor(bflat, bflat, brow2[:, :], ALU.subtract))
            dve.tensor_copy(biasb[0:1, :], brow1[0:1, :])
            dve.tensor_copy(biasb[32:33, :], brow2[32:33, :])
            dve.tensor_copy(biasb[64:65, :], bflat[64:65, :])
            link(dve.tensor_reduce(ws2m[:, :], ws2[:, :], AX_X, ALU.add))
            link(dve.tensor_scalar(ws2m[:, :], ws2m[:, :], 1.0 / D, None, ALU.mult))
            dve.tensor_scalar(ws2[:, :], ws2[:, :], ws2m[:, 0:1], None, ALU.subtract)
            dve.wait_ge(consts, 2)
            dve.tensor_copy(identb[:, :], ident[:, :])
            dve.wait_ge(iotas, 1)
            for h in range(2):
                dve.tensor_copy(iota_w[:, h * W:(h + 1) * W], iota_i[:, 0:W])
            dve.wait_ge(cut_exp, 1)
            link(dve.tensor_scalar(cutT[:, :], cutT[:, :], 1.0, None, ALU.add))
            link(dve.reciprocal(cutT[:, :], cutT[:, :]))
            for p0, p1 in ((REM // 2, 64), (64, P)):
                if p0 < p1:
                    link(dve.memset(cutT[p0:p1, NT - 2:NT], 0.0))
            dve.wait_ge(w_loaded, 16)
            link(dve.tensor_tensor(relT[:, :].rearrange("p (r j) -> p r j", j=2),
                                   dstT[:, :].rearrange("p (r j) -> p r j", j=2),
                                   w_all[:, :].unsqueeze(2).broadcast_to([P, NPAIR, 2]), ALU.subtract))
            dve.tensor_reduce(relmax[:, :], relT[:, :], AX_X, ALU.max).then_inc(relm_ready, 1)

            def table_b(g, u):
                dve.wait_ge(b1_ready, g + 1)
                for r in range(2):
                    ins = dve.tensor_tensor(rest_b[0:PB, u, r:4:2, :],
                                            ps[0:PB, 2 * u + r, 0:2 * F].rearrange("p (k f) -> p k f", f=F),
                                            stage_b[0:PB, u, r:4:2, 0:F], ALU.subtract)
                ins.then_inc(rest_ready, 1)
                dve.wait_ge(b2_ready, g + 1)
                dve.tensor_tensor(stage_b[0:PB, u, :, F:2 * F], rest_b[0:PB, u, :, :],
                                  stage_b[0:PB, u, :, 2 * F:3 * F], ALU.subtract).then_inc(tab_ready, 1)

            steps(dve, 0, NG, 2, 2, table_b)
            dve.wait_ge(relm_t, 1)
            link(dve.tensor_reduce(flagf[0:1, 0:1], ps[0:1, 0, 0:P], AX_X, ALU.max))
            dve.tensor_scalar(flag_i[0:1, 0:1], flagf[0:1, 0:1], W - 0.5, None, ALU.is_gt).then_inc(flag_ready, 1)

            link(dve.scalar_tensor_tensor(out=xs[0:PB, :, :], in0=xs[0:PB, :, :], scalar=2.0,
                                          in1=bs2r[0:PB, :].unsqueeze(1).broadcast_to([PB, NB, D]),
                                          op0=ALU.mult, op1=ALU.add))
            link(dve.tensor_reduce(xmean[0:PB, :], xs[0:PB, :, :], AX_X, ALU.add))
            link(dve.tensor_scalar(xmean[0:PB, :], xmean[0:PB, :], 1.0 / D, None, ALU.mult))
            dve.tensor_tensor(xs[0:PB, :, :], xs[0:PB, :, :],
                              xmean[0:PB, :].unsqueeze(2).broadcast_to([PB, NB, D]), ALU.subtract).then_inc(xc_ready, 1)

            def one_hot(q, u):
                if reached(q, RING):
                    dve.wait_ge(sc_mm, q - (RING - 1))
                dve.tensor_tensor(oh[:, u, :, :], iota_w[:, :].unsqueeze(1).broadcast_to([P, 4, P]),
                                  relT[:, quad_cols(q, 4, 4)].unsqueeze(2).broadcast_to([P, 4, P]),
                                  ALU.is_equal).then_inc(oh_b, 1)

            def clamp(q, u):
                dve.wait_ge(z_exp, q + 1)
                dve.tensor_scalar(ex[:, u % 2, :], ex[:, u % 2, :], CLAMP, None, ALU.min).then_inc(z_clamp, 1)

            def hidden(q, u):
                dve.wait_ge(z_ln, q + 1)
                if reached(q, 2):
                    dve.wait_ge(hg_mm, q - 1)
                dve.scalar_tensor_tensor(out=hid[:, u % 2, 0:QUAD], in0=ps[:, 2 * (u % 2), :], scalar=LN2,
                                         in1=lg[:, u % 2, 0:QUAD], op0=ALU.subtract, op1=ALU.max)
                dve.scalar_tensor_tensor(out=hid[:, u % 2, QUAD:QUAD + PAIR], in0=ps[:, 2 * (u % 2) + 1, 0:PAIR],
                                         scalar=be1l[:, 0:1], in1=lg[:, u % 2, QUAD:QUAD + PAIR],
                                         op0=ALU.add, op1=ALU.max).then_inc(hid_b, 1)

            def message(q, u, scattered=sc_mm):
                dve.wait_ge(hg_mm, q + 1)
                dve.tensor_tensor(gcut[:, :].rearrange("p (t d) -> p t d", d=D),
                                  ps_hg[:, PAIR:2 * PAIR].rearrange("p (t d) -> p t d", d=D),
                                  cutT[:, quad_cols(q, 4, 4)].unsqueeze(2).broadcast_to([P, 4, D]),
                                  ALU.mult).then_inc(gc_b, 1)
                dve.wait_ge(gc_b, q + 1)
                if scattered is not None:
                    if reached(q, 2):
                        dve.wait_ge(scattered, q - 1)
                dve.tensor_tensor(msg[:, u % 2, :, :].rearrange("p t d -> p (t d)"), ps_hg[:, 0:PAIR],
                                  gcut[:, :], ALU.mult).then_inc(msg_b, 1)

            firsts = [None] * 4

            def load_firsts(q):
                _, firsts[:] = nc.values_load_multi_w_load_instructions(
                    w_all[0:1, bass.ds(q * 2, 4)], engines=(mybir.EngineType.DVE,), min_val=0, max_val=N - W)

            def flush(q, u):
                dve.wait_ge(sc_mm, q + 1)
                if reached(q, 1):
                    dve.wait_ge(flushed, q)
                for k in range(2):
                    w = firsts[2 * (u % 2) + k]
                    half = slice(k * D, (k + 1) * D)
                    ins = dve.tensor_tensor(acc[half, bass.ds(w, W)], acc[half, bass.ds(w, W)],
                                            ps_s[half, 0:W], ALU.add)
                ins.then_inc(flushed, 1)

            def fast_step(s, u):
                known = isinstance(s, int)
                if known and s == 0:
                    one_hot(0, 0)
                    one_hot(1, 1)
                if u % 2 == 0 and (not known or 2 <= s <= NQ):
                    load_firsts(s - 2)
                if known and s == NQ + 1 and NQ % 2 == 1:
                    firsts[0:2] = [dve.value_load(w_all[0:1, NPAIR - 2 + k:NPAIR - 1 + k], min_val=0, max_val=N - W)
                                   for k in range(2)]
                if not known or s < NQ:
                    clamp(s, u)
                if not known or s + 2 < NQ:
                    one_hot(s + 2, (u + 2) % RING)
                if not known or s >= 2:
                    flush(s - 2, (u - 2) % RING)
                if not known or 1 <= s <= NQ:
                    message(s - 1, (u - 1) % RING)
                if not known or s < NQ:
                    hidden(s, u)

            def general_step(q, u):
                clamp(q, u)
                hidden(q, u)
                message(q, u, None)
                link2 = q * (SB // 2)
                dve.tensor_copy(gen_rel[:, 0, :], dstT[:, quad_cols(q, 4, 4)]).then_inc(g_rel, 1)
                with dve.Fori(0, SB // 2) as b:
                    for k in range(2):
                        done = q * SB + b * 2 + k + 2 + q
                        dve.wait_ge(g_rel, done)
                        dve.tensor_tensor(gen_oh[:, k, :, :], iota_n[:, :].unsqueeze(1).broadcast_to([P, 4, P]),
                                          gen_rel[:, k, :].unsqueeze(2).broadcast_to([P, 4, P]),
                                          ALU.is_equal).then_inc(g_oh[k], 1)
                        dve.tensor_scalar(gen_rel[:, 1 - k, :], gen_rel[:, k, :], float(P), None,
                                          ALU.subtract).then_inc(g_rel, 1)
                        dve.wait_ge(g_mm[k], link2 + b + 1)
                        dve.wait_ge(g_add[1 - k], link2 + b + 1)
                        cols = bass.ds((b * 2 + k) * P, P)
                        dve.tensor_tensor(acc[0:D, cols], acc[0:D, cols], ps_s[0:D, 0:P],
                                          ALU.add).then_inc(g_add[k], 1)
                dve.memset(flagf[0:1, 1:2], 0.0).then_inc(flushed, 1)

            dve.wait_ge(acc_zeroed, 1)
            general = general_of(dve)
            with dve.If(general):
                dve.tensor_copy(relT[:, :].bitcast(I32), dstT[:, :]).then_inc(g_rel, 1)
                dve.memset(flagf[0:1, 1:2], 0.0).then_inc(g_add[1], 1)
                steps(dve, 0, NQ, RING, RING, general_step, tail=1)
            with dve.Else():
                steps(dve, 0, NQ + 2, RING, RING, fast_step, tail=4)

            def node_clamp(k, u):
                dve.wait_ge(n_mm, k + 1)
                if reached(k, 2):
                    dve.wait_ge(n_ln, k - 1)
                dve.tensor_scalar(ex[:, u, 0:2 * PB], ps[:, u, 0:2 * PB], bs1c[:, 0:1], ZMAX, ALU.add,
                                  ALU.min).then_inc(n_clamp, 1)

            def node_max(k, u):
                dve.wait_ge(n_ln, k + 1)
                if reached(k, 2):
                    dve.wait_ge(y_mm, k - 1)
                dve.scalar_tensor_tensor(out=hid[:, u, 0:2 * PB], in0=ps[:, u, 0:2 * PB], scalar=bs1l[:, 0:1],
                                         in1=lg[:, u, 0:2 * PB], op0=ALU.add, op1=ALU.max).then_inc(n_hid, 1)

            def node_add(k, u):
                dve.wait_ge(y_mm, k + 1)
                if reached(k, 2):
                    dve.wait_ge(y_out, k - 1)
                dve.tensor_tensor(dd[0:PB, u, :, :].rearrange("p (h c) d -> p h (c d)", h=2),
                                  ps[0:PB, 4 + 2 * u:6 + 2 * u, 0:2 * D],
                                  xs[0:PB, bass.ds(k * 4, 4), :].rearrange("p (h c) d -> p h (c d)", h=2),
                                  ALU.add).then_inc(y_add, 1)

            def node_sum(k, u):
                dve.wait_ge(y_sq, k + 1)
                dve.tensor_reduce(ssum[0:PB, u, :], sq[0:PB, u, :, :], AX_X, ALU.add).then_inc(y_sum, 1)

            def node_scale(k, u):
                dve.wait_ge(y_rstd, k + 1)
                if reached(k, 2):
                    dve.wait_ge(s_out[u], per_ring(k, u, 2, 16) - 16)
                dve.tensor_tensor(outs[0:PB, u, :, :], dd[0:PB, u, :, :],
                                  rstd[0:PB, u, :].unsqueeze(2).broadcast_to([PB, 4, D]),
                                  ALU.mult).then_inc(y_out, 1)

            def node_step(k, u):
                known = isinstance(k, int)
                if not known or k < NG:
                    node_clamp(k, u)
                if not known or k < NG:
                    node_max(k, u)
                if not known or k >= 1:
                    node_add(k - 1, (u - 1) % 2)
                    node_sum(k - 1, (u - 1) % 2)
                    node_scale(k - 1, (u - 1) % 2)

            steps(dve, 0, NG + 1, 2, 2, node_step, tail=1)


_INS = ["x", "src", "dst", "edge_attr_64", "edge_weight1"] + [
    "L0_gnn_" + n for n in ("We1", "be1", "We2", "be2", "Wn1", "bn1", "Wn2", "bn2", "Ws1", "bs1", "Ws2", "bs2")]


def kernel(**inputs):
    import numpy as _np
    import concourse.bacc as _bacc
    from concourse import mybir as _mybir
    from concourse.bass_utils import run_bass_kernel_spmd as _run

    nc = _bacc.Bacc("TRN2", target_bir_lowering=False, num_devices=1)
    arrays, args = {}, []
    for name in _INS:
        a = _np.ascontiguousarray(inputs[name])
        arrays[f"in_{name}_dram"] = a
        args.append(nc.dram_tensor(f"in_{name}_dram", a.shape, _mybir.dt.from_np(a.dtype), kind="ExternalInput").ap())
    n, d = inputs["x"].shape
    out = nc.dram_tensor("out_0_dram", (n, d), _mybir.dt.float32, kind="ExternalOutput").ap()
    gnn_layer(nc, *args, out)
    r = _run(nc, [arrays], core_ids=[0])
    return r.results[0]["out_0_dram"]
```

```python
from contextlib import ExitStack

import numpy as np
import concourse.bass as bass
from concourse import mybir
from concourse.alu_op_type import AluOpType as ALU

F32 = mybir.dt.float32
BF16 = mybir.dt.bfloat16
I32 = mybir.dt.int32
ACT = mybir.ActivationFunctionType
AX_X = mybir.AxisListType.X
LN2 = float(np.log(2.0))

P = 128
PAIR = 2 * P
QUAD = 2 * PAIR
W = 64
RING = 4
ARING = 8
IRING = ARING // 2
STAGES = 4
CLAMP = 1e17
ZMAX = 40.0
EPS = 1e-5


def reached(i, n):
    return not isinstance(i, int) or i >= n


def steps(eng, first, last, peel, unroll, body, tail=0):
    start = first + peel
    assert start % unroll == 0
    stop = start + max(0, (last - tail - start) // unroll * unroll)
    for i in range(first, min(start, last)):
        body(i, i % unroll)
    if stop > start:
        with eng.Fori(start, stop - unroll + 1, unroll) as base:
            for u in range(unroll):
                body(base + u, u)
    for i in range(stop, last):
        body(i, i % unroll)


def per_ring(i, u, ring, count):
    if isinstance(i, int):
        return count * (i // ring + 1)
    return (i - u + ring) * (count // ring)


def gnn_layer(nc, x, src, dst, edge_attr, dist, We1, be1, We2, be2, Wn1, bn1, Wn2, bn2,
              Ws1, bs1, Ws2, bs2, out):
    N, D = x.shape
    E = src.shape[0]
    F = 2 * D
    assert D == 64 and F == P and N > W

    PB = 125
    NB = N // PB
    assert PB * NB == N and NB % 4 == 0
    NG = NB // 4
    SB = -(-N // P)
    SB += SB % 2
    NQ = -(-E // QUAD)
    NPAIR = 2 * NQ
    FULL = E // PAIR
    REM = E - FULL * PAIR
    assert FULL == NPAIR - 1 and REM > 0 and PAIR % REM == 0 and REM % 64 == 0
    NT = 2 * NPAIR
    RG = -(-NPAIR // P)
    RL = NPAIR - (RG - 1) * P

    with ExitStack() as ctx:
        ctx.enter_context(nc.allow_non_contiguous_dma(reason="small tables"))

        def sb(name, shape, dt=F32):
            return ctx.enter_context(nc.sbuf_tensor(name, shape, dt))

        def sem(name):
            return ctx.enter_context(nc.semaphore(name))

        a_tab = nc.dram_tensor("a_tab", (N, F), F32, kind="Internal").ap()
        b_tab = nc.dram_tensor("b_tab", (N, 4 * F), BF16, kind="Internal").ap()
        w_tab = nc.dram_tensor("w_tab", (1, RG * P), I32, kind="Internal").ap()

        ident = sb("ident", [P, P])
        identb = sb("identb", [P, P], BF16)
        iota_i = sb("iota_i", [P, P], I32)
        iota_w = sb("iota_w", [P, P])
        iota_n = sb("iota_n", [P, P])
        ones_b = sb("ones_b", [P, P], BF16)
        we1 = sb("we1", [P, P])
        we2 = sb("we2", [P, P])
        wn1 = sb("wn1", [P, 2, F])
        wn2 = sb("wn2", [P, D])
        ws1 = sb("ws1", [P, D])
        ws2 = sb("ws2", [P, D])
        ws2m = sb("ws2m", [P, 1])
        be1c = sb("be1c", [P, 1])
        be1l = sb("be1l", [P, 1])
        bs1c = sb("bs1c", [P, 1])
        bs1l = sb("bs1l", [P, 1])
        bn1r = sb("bn1r", [P, F])
        bs2r = sb("bs2r", [P, D])
        brow = sb("brow", [P, 2, 4, D])
        brow1 = sb("brow1", [P, QUAD], BF16)
        brow2 = sb("brow2", [P, QUAD], BF16)
        biasb = sb("biasb", [P, QUAD], BF16)
        cexp = sb("cexp", [P, 1])
        epsc = sb("epsc", [P, 1])
        halfc = sb("halfc", [P, 1])

        acc = sb("acc", [P, SB * P])
        RI, RF = 2 * RG * PAIR, 3 * RG * PAIR
        assert RI + RF <= SB * P
        rows_i = acc[:, 0:RI].bitcast(I32).rearrange("p (k g e) -> p k g e", k=2, e=PAIR)
        rows_f = acc[:, RI:RI + RF].rearrange("p (k g e) -> p k g e", k=3, e=PAIR)
        dmin = sb("dmin", [P, RG])
        w_i = sb("w_i", [P, RG], I32)
        w_all = sb("w_all", [P, NPAIR], I32)
        srcT = sb("srcT", [P, NT], I32)
        dstT = sb("dstT", [P, NT])
        relT = sb("relT", [P, NT])
        cutT = sb("cutT", [P, NT])
        relmax = sb("relmax", [P, 1])
        flagf = sb("flagf", [1, 2])
        flag_i = sb("flag_i", [1, 2], I32)

        xs = sb("xs", [P, NB, D])
        xmean = sb("xmean", [P, NB])
        bmean = sb("bmean", [P, 1])

        region_a = sb("region_a", [P, STAGES * 4 * F])
        stage_a = region_a[:, :].rearrange("p (u b f) -> p u b f", u=STAGES, f=F)
        hid = region_a[:, 0:2 * (QUAD + PAIR)].rearrange("p (u e) -> p u e", u=2)
        msg = region_a[:, 2 * (QUAD + PAIR):2 * (QUAD + PAIR) + 8 * D].rearrange("p (u t d) -> p u t d", u=2, d=D)
        region_r = sb("region_r", [P, 2 * 4 * F])
        rest_b = region_r[:, :].rearrange("p (u b f) -> p u b f", u=2, f=F)
        eaT = region_r[:, 0:2 * PAIR].rearrange("p (u e) -> p u e", u=2)
        ohT = region_r[:, 2 * PAIR:2 * PAIR + QUAD].bitcast(BF16).rearrange("p (u e) -> p u e", u=2)
        region_b = sb("region_b", [P, STAGES * 4 * 2 * F])
        stage_b = region_b[:, :].bitcast(BF16).rearrange("p (u b f) -> p u b f", u=STAGES, b=4)
        oh = region_b[:, 0:RING * 4 * P].rearrange("p (u t w) -> p u t w", u=RING, w=P)
        dd, sq, outs = (region_b[:, k0:k0 + n * 4 * D].rearrange("p (u b d) -> p u b d", u=n, d=D)
                        for k0, n in ((RING * 4 * P, 4), (RING * 4 * P + 16 * D, 2), (RING * 4 * P + 24 * D, 2)))

        idxb = sb("idxb", [P, IRING, 8], I32)
        ea = sb("ea", [P, RING, 2, P])
        ga = sb("ga", [P, ARING, 4, F])
        bw = sb("bw", [P, RING, 2, 2, F], BF16)
        gcut = sb("gcut", [P, PAIR])

        late_words = 2 * 2 * (QUAD + PAIR) + 8 + 8 + 2 * 4 * P + 4 * 4 * F // 2
        shared = sb("shared", [P, max(NB // 2 * PB, late_words)])
        xT = shared[:, 0:NB // 2 * PB].rearrange("p (k c) -> p k c", c=PB)
        taken = [0]

        def late(shape, dt=F32):
            words = int(np.prod(shape)) // (2 if dt == BF16 else 1)
            part = shared[:, taken[0]:taken[0] + words]
            taken[0] += words
            if dt != F32:
                part = part.bitcast(dt)
            names = "abc"[:len(shape)]
            return part.rearrange(f"p ({' '.join(names)}) -> p {' '.join(names)}", **dict(zip(names, shape)))

        ex = late([2, QUAD + PAIR])
        lg = late([2, QUAD + PAIR])
        gen_idx = late([8], I32)
        gen_rel = late([2, 4])
        gen_oh = late([2, 4, P])
        gen_b = late([4, 4 * F], BF16)
        assert taken[0] <= late_words

        ssum = sb("ssum", [P, 2, 4])
        lvar = sb("lvar", [P, 2, 4])
        rstd = sb("rstd", [P, 2, 4])

        ps = ctx.enter_context(nc.psum_tensor("ps", [P, 8, 512], F32))
        ps_eaT, ps_ohT, ps_hg, ps_s = ps[:, 4, :], ps[:, 5, :], ps[:, 6, :], ps[:, 7, :]

        ld_src, ld_dst, ld_dist, ld_x, ld_wn, ld_w, ld_bd = (sem(n) for n in (
            "ld_src", "ld_dst", "ld_dist", "ld_x", "ld_wn", "ld_w", "ld_bd"))
        zeroed, consts, iotas, dve_chain, act_chain = (sem(n) for n in (
            "zeroed", "consts", "iotas", "dve_chain", "act_chain"))
        rows_ready = [sem(f"rows_ready{k}") for k in range(2)]
        row_t, row_dve, row_act = sem("row_t"), sem("row_dve"), sem("row_act")
        acc_zeroed = sem("acc_zeroed")
        w_ready, w_stored, w_loaded = sem("w_ready"), sem("w_stored"), sem("w_loaded")
        relm_ready, relm_t, flag_ready = sem("relm_ready"), sem("relm_t"), sem("flag_ready")
        cut_exp = sem("cut_exp")
        xT_t, xT_e = sem("xT_t"), sem("xT_e")
        tab_mm, tab_ready = sem("tab_mm"), sem("tab_ready")
        b1_ready, rest_ready, b2_ready = sem("b1_ready"), sem("rest_ready"), sem("b2_ready")
        a_stored = [sem(f"a_stored{k}") for k in range(STAGES)]
        b_stored = [sem(f"b_stored{k}") for k in range(STAGES)]
        quads_begun = sem("quads_begun")
        s_idx = [sem(f"s_idx{k}") for k in range(IRING)]
        s_ea = [sem(f"s_ea{k}") for k in range(RING)]
        s_ga = [sem(f"s_ga{k}") for k in range(ARING)]
        s_bw = [sem(f"s_bw{k}") for k in range(RING)]
        ea_t, ea_e, oh_b, oh_t, oh_e, z_mm, z_exp, z_clamp, z_ln, hid_b, hg_mm, gc_b, msg_b, sc_mm, flushed = (
            sem(n) for n in ("ea_t", "ea_e", "oh_b", "oh_t", "oh_e", "z_mm", "z_exp", "z_clamp", "z_ln",
                             "hid_b", "hg_mm", "gc_b", "msg_b", "sc_mm", "flushed"))
        g_idx, g_b = sem("g_idx"), sem("g_b")
        g_rel = sem("g_rel")
        g_oh = [sem(f"g_oh{k}") for k in range(2)]
        g_mm = [sem(f"g_mm{k}") for k in range(2)]
        g_add = [sem(f"g_add{k}") for k in range(2)]
        n_mm, n_exp, n_clamp, n_ln, n_hid, y_mm, y_add, y_sq, y_sum, y_lv, y_rstd, y_out = (
            sem(n) for n in ("n_mm", "n_exp", "n_clamp", "n_ln", "n_hid", "y_mm", "y_add", "y_sq", "y_sum",
                             "y_lv", "y_rstd", "y_out"))
        x_sum, xc_ready = sem("x_sum"), sem("xc_ready")
        s_out = [sem(f"s_out{k}") for k in range(2)]

        block = ctx.enter_context(nc.Block())

        N_LD_W = 10
        N_LD_ROWS = (RG > 1) + 2
        G1 = 4
        G2 = min(12, NG // 4 * 4)
        assert NG >= 8

        def uses(slot, slots):
            return (NG - slot + slots - 1) // slots

        def row_views(t):
            full = t[0:FULL * PAIR].rearrange("(r e) -> r e", e=PAIR)
            head = None
            if RG > 1:
                head = full[0:(RG - 1) * P, :].rearrange("(g p) e -> p g e", p=P)
            return head, full[(RG - 1) * P:FULL, :], t[FULL * PAIR:E].rearrange("(r e) -> r e", r=1)

        def quad_cols(i, size, scale):
            return bass.ds(i * scale, size)

        def general_of(eng):
            eng.wait_ge(flag_ready, 1)
            return eng.value_load(flag_i[0:1, 0:1], min_val=0, max_val=1)

        @block.sync
        def _(sp):
            def load_rows(t, to, done):
                head, tail, rest = row_views(t)
                if head is not None:
                    sp.dma_start(to[:, 0:RG - 1, :], head).then_inc(done, 16)
                sp.dma_start(to[0:RL - 1, RG - 1, :], tail).then_inc(done, 16)
                sp.dma_start(to[RL - 1:RL, RG - 1, :].rearrange("r (k e) -> r k e", e=REM),
                             rest.unsqueeze(1).broadcast_to([1, PAIR // REM, REM])).then_inc(done, 16)

            sp.dma_start(xs[0:PB, :, :], x.rearrange("(p b) d -> p b d", b=NB)).then_inc(ld_x, 16)
            sp.dma_start(wn1[0:D, :, :], Wn1.rearrange("(h k) f -> k h f", h=2)).then_inc(ld_wn, 16)
            sp.dma_start(wn1[D:P, :, :], Wn1.rearrange("(h k) f -> k h f", h=2)).then_inc(ld_wn, 16)
            sp.dma_start(bn1r[:, :], bn1.rearrange("(a f) -> a f", a=1).broadcast_to([P, F])).then_inc(ld_wn, 16)
            row = lambda v: v.rearrange("(a f) -> a f", a=1)
            sp.dma_start(bs2r[:, :], row(bs2).broadcast_to([P, D])).then_inc(ld_wn, 16)
            load_rows(src, rows_i[:, 0], ld_src)
            load_rows(dst, rows_i[:, 1], ld_dst)
            load_rows(dist.rearrange("e a -> (e a)"), rows_f[:, 2], ld_dist)

            av = a_tab.rearrange("(p b) f -> p b f", b=NB)
            bv = b_tab.rearrange("(p b) f -> p b f", b=NB)

            def store_a(g, u):
                sp.wait_ge(tab_ready, g + 1)
                sp.dma_start(av[:, bass.ds(g * 4, 4), :], stage_a[0:PB, u, :, :]).then_inc(a_stored[u], 16)

            def store_b(g, u):
                sp.wait_ge(tab_ready, g + (NG + 1))
                sp.dma_start(bv[:, bass.ds(g * 4, 4), :], stage_b[0:PB, u, :, :]).then_inc(b_stored[u], 16)

            steps(sp, 0, G1, G1, STAGES, store_a)

            sp.wait_ge(row_dve, RG)
            for slot in range(IRING):
                sp.dma_start(idxb[:, slot, :], srcT[:, slot * 8:slot * 8 + 8]).then_inc(s_idx[slot], 16)

            sp.wait_ge(w_ready, 1)
            wv = w_tab.rearrange("a (g p) -> p (a g)", p=P)
            if RG > 1:
                sp.dma_start(wv[:, 0:RG - 1], w_i[:, 0:RG - 1]).then_inc(w_stored, 16)
            sp.dma_start(wv[0:RL, RG - 1:RG], w_i[0:RL, RG - 1:RG]).then_inc(w_stored, 16)
            sp.wait_ge(w_stored, 16 * (1 + (RG > 1)))
            sp.dma_start(w_all[:, :], w_tab[:, 0:NPAIR].broadcast_to([P, NPAIR])).then_inc(w_loaded, 16)

            col = lambda v: v.rearrange("(f a) -> f a", a=1)
            sp.wait_ge(zeroed, 1)
            for h in range(2):
                half = slice(h * D, (h + 1) * D)
                sp.dma_start(we1[half, half], We1).then_inc(ld_bd, 16)
                sp.dma_start(we2[half, half], We2).then_inc(ld_bd, 16)
            for r in (0, 32, 64):
                for h, v in enumerate((bn2, be2)):
                    sp.dma_start(brow[r:r + 1, h, :, :],
                                 row(v).unsqueeze(1).broadcast_to([1, 4, D])).then_inc(ld_bd, 16)
            for h in range(2):
                half = slice(h * D, (h + 1) * D)
                sp.dma_start(be1c[half, :], col(be1)).then_inc(ld_w, 16)
                sp.dma_start(bs1c[half, :], col(bs1)).then_inc(ld_w, 16)
                sp.dma_start(ws1[half, :], Ws1).then_inc(ld_w, 16)
                sp.dma_start(ws2[half, :], Ws2).then_inc(ld_w, 16)
            sp.dma_start(wn2[0:D, :], Wn2[0:D, :]).then_inc(ld_w, 16)
            sp.dma_start(wn2[D:P, :], Wn2[D:P, :]).then_inc(ld_w, 16)

            steps(sp, G1, NG, 0, STAGES, store_a)

            def load_ea(q, u):
                if reached(q, RING):
                    sp.wait_ge(ea_t, q - (RING - 1))
                if isinstance(q, int) and q == NQ - 1:
                    full = edge_attr[q * QUAD:q * QUAD + PAIR, :].rearrange("(p j) d -> p (j d)", j=2)
                    sp.dma_start(ea[:, u, 0, :], full).then_inc(s_ea[u], 8 * 2)
                    part = edge_attr[FULL * PAIR:E, :].rearrange("(p j) d -> p (j d)", j=2)
                    sp.dma_start(ea[0:REM // 2, u, 1, :], part).then_inc(s_ea[u], 16)
                else:
                    rows = edge_attr[bass.ds(q * QUAD, QUAD), :]
                    sp.dma_start(ea[:, u, :, :], rows.rearrange("(k p j) d -> p k (j d)", p=P, j=2)).then_inc(s_ea[u], 16)

            firsts = [None] * 4

            def fast_step(q, v):
                u = v % RING
                if v % 2 == 0:
                    if not isinstance(q, int) or RING <= q < NQ - RING:
                        for k in (4, 3):
                            sp.wait_ge(s_ga[(v - k) % ARING], per_ring(q - k, (v - k) % ARING, ARING, 64))
                        slot = (v // 2 + 2) % IRING
                        n = 8 if not isinstance(q, int) or q + 5 < NQ else 4
                        sp.dma_start(idxb[:, slot, 0:n], srcT[:, quad_cols(q + 4, n, 4)]).then_inc(s_idx[slot], 16)
                    if isinstance(q, int) and q + 1 == NQ:
                        firsts[0:2] = [sp.value_load(w_all[0:1, q * 2 + k:q * 2 + k + 1], min_val=0, max_val=N - W)
                                       for k in range(2)]
                    else:
                        _, firsts[:] = nc.values_load_multi_w_load_instructions(
                            w_all[0:1, bass.ds(q * 2, 4)], engines=(mybir.EngineType.SP,), min_val=0, max_val=N - W)
                if reached(q, RING):
                    load_ea(q, u)
                if reached(q, RING):
                    sp.wait_ge(z_mm, q - (RING - 1))
                for k in range(2):
                    rows = b_tab[bass.ds(firsts[2 * (v % 2) + k], W), :].rearrange("w (h cf) -> h w cf", h=2)
                    sp.dma_start(bw[:, u, k, :, :].rearrange("p c f -> p (c f)"), rows).then_inc(s_bw[u], 16)

            def general_step(q, u):
                if reached(q, 1):
                    sp.wait_ge(s_ga[0], q * 64)
                if reached(q, 1):
                    sp.wait_ge(g_b, q * 64)
                sp.dma_start(gen_idx[:, 0:4], srcT[:, quad_cols(q, 4, 4)]).then_inc(g_idx, 16)
                sp.dma_start(gen_idx[:, 4:8], gen_dst[:, quad_cols(q, 4, 4)]).then_inc(g_idx, 16)
                if reached(q, RING):
                    load_ea(q, u)

            gen_dst = relT[:, :].bitcast(I32)
            for q in range(RING):
                load_ea(q, q)
            steps(sp, 0, NG, STAGES, STAGES, store_b)
            general = general_of(sp)
            for k in range(STAGES):
                sp.wait_ge(b_stored[k], 16 * uses(k, STAGES))
            with sp.If(general):
                sp.wait_ge(g_rel, 1)
                steps(sp, 0, NQ, RING, RING, general_step, tail=1)
            with sp.Else():
                steps(sp, 0, NQ, ARING, ARING, fast_step, tail=RING + 2)

            ov = out.rearrange("(p b) d -> p b d", b=NB)

            def store_out(k, u):
                sp.wait_ge(y_out, k + 1)
                sp.dma_start(ov[:, bass.ds(k * 4, 4), :], outs[0:PB, u, :, :]).then_inc(s_out[u], 16)

            steps(sp, 0, NG, 2, 2, store_out)
            for k in range(2):
                sp.wait_ge(s_out[k], 16 * uses(k, 2))

        @block.gpsimd
        def _(pool):
            pool.memset(ident[:, :], 0.0).then_inc(consts, 1)
            pool.wait_ge(consts, 1)
            pool.affine_select(out=ident[:, :], in_=ident[:, :], compare_op=ALU.not_equal, fill=1.0,
                               base=0, pattern=[[-1, P]], channel_multiplier=1).then_inc(consts, 1)
            pool.iota(iota_i[:, :], pattern=[[1, P]], base=0, channel_multiplier=0).then_inc(iotas, 1)

            pool.wait_ge(row_t, 3 * RG)
            pool.wait_ge(w_ready, 1)
            pool.memset(acc[:, :], 0.0).then_inc(acc_zeroed, 1)

            def gather_rows(to, table, idx, done):
                pool.sem_inc(quads_begun, 1)
                for t in range(4):
                    pool.indirect_dma_start(to[:, t, :], None, table,
                                            bass.IndirectOffsetOnAxis(ap=idx[:, t:t + 1], axis=0)).then_inc(done, 16)

            def fast_step(q, v):
                pool.wait_ge(s_idx[v // 2], per_ring(q, v, ARING, 16))
                if reached(q, ARING):
                    pool.wait_ge(z_mm, q - (ARING - 1))
                gather_rows(ga[:, v], a_tab, idxb[:, v // 2, 4 * (v % 2):4 * (v % 2) + 4], s_ga[v])

            def general_step(q, u):
                pool.wait_ge(g_idx, q * 32 + 32)
                if reached(q, 1):
                    pool.wait_ge(z_mm, q)
                gather_rows(ga[:, 0], a_tab, gen_idx[:, 0:4], s_ga[0])
                gather_rows(gen_b, b_tab, gen_idx[:, 4:8], g_b)

            general = general_of(pool)
            for k in range(STAGES):
                pool.wait_ge(a_stored[k], 16 * uses(k, STAGES))
            with pool.If(general):
                for k in range(STAGES):
                    pool.wait_ge(b_stored[k], 16 * uses(k, STAGES))
                steps(pool, 0, NQ, RING, RING, general_step, tail=1)
            with pool.Else():
                steps(pool, 0, NQ, ARING, ARING, fast_step)

        @block.tensor
        def _(pe):
            pe.wait_ge(consts, 2)

            def transpose_rows():
                for k in range(3):
                    if k < 2:
                        pe.wait_ge(rows_ready[k], 1)
                    else:
                        pe.wait_ge(ld_dist, 16 * N_LD_ROWS)
                    for g in range(RG):
                        n = k * RG + g
                        rows = P if g < RG - 1 else RL
                        if n >= 2:
                            if n - 2 < RG:
                                pe.wait_ge(row_dve, n - 1)
                            else:
                                pe.wait_ge(row_act, n - 1 - RG)
                        for j in range(2):
                            mm = pe.transpose(ps[:, 6 + n % 2, j * P:j * P + rows],
                                              rows_f[0:rows, k, g, j:PAIR:2], ident[0:rows, 0:rows])
                        mm.then_inc(row_t, 1)

            pe.wait_ge(ld_x, 16)
            pe.wait_ge(ld_wn, 16 * 4)

            def transpose_x(g):
                if g >= 2:
                    pe.wait_ge(xT_e, g - 1)
                for k in range(2):
                    blocks = xs[0:PB, g * 4 + 2 * k:g * 4 + 2 * k + 2, :].rearrange("p b d -> p (b d)")
                    mm = pe.transpose(ps[:, 4 + g % 2, k * PB:(k + 1) * PB], blocks, ident[0:PB, 0:PB])
                mm.then_inc(xT_t, 1)

            def table_mm(g, half, bank):
                for par in range(2):
                    rows = slice(par * D, (par + 1) * D)
                    for k in range(2):
                        mm = pe.matmul(ps[0:PB, bank + par, k * F:(k + 1) * F], xT[rows, g * 2 + k, :],
                                       wn1[rows, half, :], start=True, stop=True)
                mm.then_inc(tab_mm, 1)

            transpose_x(0)
            for g in range(NG):
                if g + 1 < NG:
                    transpose_x(g + 1)
                pe.wait_ge(xT_e, g + 1)
                if g >= 2:
                    pe.wait_ge(tab_ready, g - 1)
                table_mm(g, 0, 2 * (g % 2))
                if g == G1 - 1:
                    transpose_rows()

            pe.wait_ge(row_act, 2 * RG)
            pe.wait_ge(relm_ready, 1)
            pe.transpose(ps[0:1, 6, 0:P], relmax[:, 0:1], ident[:, :]).then_inc(relm_t, 1)
            for g in range(NG):
                if g == 0:
                    pe.wait_ge(tab_ready, NG)
                if g == 3:
                    pe.wait_ge(flag_ready, 1)
                if g >= 4:
                    pe.wait_ge(rest_ready, g - 3)
                table_mm(g, 1, 2 * (g % 4))
            pe.wait_ge(rest_ready, NG)
            pe.wait_ge(ld_bd, 16 * 10)
            pe.wait_ge(ld_w, 16 * N_LD_W)

            def transpose_ea(q, u):
                pe.wait_ge(s_ea[u], per_ring(q, u, RING, 16) + (16 if isinstance(q, int) and q == NQ - 1 else 0))
                if reached(q, 1):
                    pe.wait_ge(ea_e, q)
                for k in range(2):
                    mm = pe.transpose(ps_eaT[:, k * P:(k + 1) * P], ea[:, u, k, :], ident[:, :])
                mm.then_inc(ea_t, 1)

            def source_part(q, u, slot, landed):
                pe.wait_ge(s_ga[slot], landed)
                if reached(q, 2):
                    pe.wait_ge(hid_b, q - 1)
                z = ps[:, 2 * (u % 2), :]
                for t in range(4):
                    pe.matmul(z[:, t * P:(t + 1) * P], ga[:, slot, t, :], ident[:, :], is_transpose=True,
                              start=(t == 0), stop=False, skip_group_check=True)

            def gate_part(q, u):
                pe.wait_ge(ea_e, q + 1)
                pe.matmul(ps[:, 2 * (u % 2) + 1, 0:PAIR], we1[:, :], eaT[:, u % 2, :], start=True, stop=True)

            def transposes(q, u):
                transpose_ea(q, u)
                pe.wait_ge(oh_b, q + 1)
                if reached(q, 1):
                    pe.wait_ge(oh_e, q)
                for t in range(4):
                    mm = pe.transpose(ps_ohT[:, t * P:(t + 1) * P], oh[:, u, t, :], ident[:, :])
                mm.then_inc(oh_t, 1)

            def front(q, v):
                u = v % RING
                source_part(q, u, v, per_ring(q, v, ARING, 64))
                gate_part(q, u)
                pe.wait_ge(oh_e, q + 1)
                pe.wait_ge(s_bw[u], per_ring(q, u, RING, 32))
                z = ps[:, 2 * (u % 2), :]
                for k in range(2):
                    for c in range(2):
                        cols = slice(k * PAIR, (k + 1) * PAIR)
                        mm = pe.matmul(z[:, cols], bw[:, u, k, c, :], ohT[:, u % 2, cols],
                                       start=False, stop=(c == 1), skip_group_check=True)
                mm.then_inc(z_mm, 1)

            def mid(q, u):
                pe.wait_ge(hid_b, q + 1)
                if reached(q, 1):
                    pe.wait_ge(msg_b, q)
                pe.matmul(ps_hg[:, :], ones_b[:, :], biasb[:, :], start=True, stop=False, skip_group_check=True)
                for t in range(4):
                    pe.matmul(ps_hg[:, t * D:(t + 1) * D], hid[:, u % 2, t * P:(t + 1) * P], wn2[:, :],
                              start=False, stop=False, skip_group_check=True)
                for k in range(2):
                    mm = pe.matmul(ps_hg[:, PAIR + k * P:PAIR + (k + 1) * P],
                                   hid[:, u % 2, QUAD + k * P:QUAD + (k + 1) * P], we2[:, :],
                                   start=False, stop=(k == 1), skip_group_check=True)
                mm.then_inc(hg_mm, 1)

            def back(q, u):
                pe.wait_ge(msg_b, q + 1)
                if reached(q, 1):
                    pe.wait_ge(flushed, q)
                for k in range(2):
                    for j in range(2):
                        mm = pe.matmul(ps_s[k * D:(k + 1) * D, 0:W], msg[:, u % 2, 2 * k + j, :],
                                       oh[:, u, 2 * k + j, 0:W], start=(j == 0), stop=(j == 1))
                mm.then_inc(sc_mm, 1)

            def fast_step(s, v):
                known = isinstance(s, int)
                u = v % RING
                if known and s == 0:
                    transposes(0, 0)
                if not known or s < NQ:
                    front(s, v)
                if not known or s + 1 < NQ:
                    transposes(s + 1, (u + 1) % RING)
                if not known or s >= 2:
                    back(s - 2, (u - 2) % RING)
                if not known or 1 <= s <= NQ:
                    mid(s - 1, (u - 1) % RING)

            def general_step(q, u):
                transpose_ea(q, u)
                source_part(q, u, 0, q * 64 + 64)
                gate_part(q, u)
                pe.wait_ge(g_b, q * 64 + 64)
                z = ps[:, 2 * (u % 2), :]
                for t in range(4):
                    for c in range(3):
                        mm = pe.matmul(z[:, t * P:(t + 1) * P], gen_b[:, t, c * F:(c + 1) * F], identb[:, :],
                                       start=False, stop=(c == 2), skip_group_check=True)
                mm.then_inc(z_mm, 1)
                mid(q, u)
                with pe.Fori(0, SB // 2) as b:
                    for k in range(2):
                        pe.wait_ge(msg_b, q + 1)
                        pe.wait_ge(g_oh[k], q * (SB // 2) + b + 1)
                        pe.wait_ge(g_add[1 - k], q * (SB // 2) + b + 1)
                        for t in range(4):
                            mm = pe.matmul(ps_s[0:D, 0:P], msg[:, u % 2, t, :], gen_oh[:, k, t, :],
                                           start=(t == 0), stop=(t == 3))
                        mm.then_inc(g_mm[k], 1)

            general = general_of(pe)
            with pe.If(general):
                steps(pe, 0, NQ, RING, RING, general_step, tail=1)
            with pe.Else():
                steps(pe, 0, NQ + 2, ARING, ARING, fast_step, tail=4)

            accv = acc[:, 0:N].rearrange("f (p b) -> f b p", b=NB)

            def node_hidden(k, u):
                if reached(k, 2):
                    pe.wait_ge(n_hid, k - 1)
                for h in range(2):
                    mm = pe.matmul(ps[h * D:(h + 1) * D, u, 0:2 * PB].rearrange("f (b p) -> f b p", b=2),
                                   ws1[:, :], accv[:, bass.ds(k * 4 + 2 * h, 2), :],
                                   start=True, stop=True)
                mm.then_inc(n_mm, 1)

            def node_out(k, u):
                pe.wait_ge(n_hid, k + 1)
                if reached(k, 2):
                    pe.wait_ge(y_add, k - 1)
                for c in range(2):
                    for h in range(2):
                        rows = slice(h * D, (h + 1) * D)
                        mm = pe.matmul(ps[0:PB, 4 + 2 * u + h, c * D:(c + 1) * D],
                                       hid[rows, u, c * PB:(c + 1) * PB], ws2[rows, :], start=True, stop=True)
                mm.then_inc(y_mm, 1)

            pe.wait_ge(flushed, NQ)
            node_hidden(0, 0)
            for k in range(1, NG + 1):
                if k >= 2:
                    node_out(k - 2, k % 2)
                if k < NG:
                    node_hidden(k, k % 2)
            node_out(NG - 1, (NG - 1) % 2)

        @block.scalar
        def _(act):
            act.preload_act_table_set("natural_log_exp_and_others")
            act.wait_ge(iotas, 1)
            act.copy(iota_n[:, :], iota_i[:, :]).then_inc(act_chain, 1)

            def evacuate_x(g, u):
                act.wait_ge(xT_t, g + 1)
                act.copy(xT[:, bass.ds(g * 2, 2), :],
                         ps[:, 4 + u, 0:2 * PB].rearrange("p (k c) -> p k c", k=2)).then_inc(xT_e, 1)

            steps(act, 0, G1, G1, 2, evacuate_x)
            act.wait_ge(ld_dst, 16 * N_LD_ROWS)
            if RG > 1:
                act.copy(rows_f[:, 1, 0:RG - 1, :], rows_i[:, 1, 0:RG - 1, :])
            act.copy(rows_f[0:RL, 1, RG - 1, :], rows_i[0:RL, 1, RG - 1, :]).then_inc(rows_ready[1], 1)
            for k, to in ((1, dstT), (2, cutT)):
                for g in range(RG):
                    n = k * RG + g
                    rows = P if g < RG - 1 else RL
                    act.wait_ge(row_t, n + 1)
                    tv = to[:, 2 * P * g:2 * (P * g + rows)].rearrange("p (r j) -> p j r", j=2)
                    pv = ps[:, 6 + n % 2, 0:PAIR].rearrange("p (j r) -> p j r", j=2)[:, :, 0:rows]
                    act.copy(tv, pv).then_inc(row_act, 1)
            steps(act, G1, NG, 0, 2, evacuate_x)
            act.wait_ge(row_act, 2 * RG)
            act.wait_ge(zeroed, 1)
            act.activation(cutT[:, :], cutT[:, :], ACT.Exp, bias=cexp[:, 0:1], scale=5.0).then_inc(cut_exp, 1)

            def split_first(g, u):
                act.wait_ge(tab_mm, g + (NG + 1))
                if reached(g, STAGES):
                    act.wait_ge(b_stored[u], per_ring(g, u, STAGES, 16) - 16)
                act.copy(stage_b[0:PB, u, :, 0:F].rearrange("p (k r) f -> p r k f", r=2),
                         ps[0:PB, 2 * u:2 * u + 2, 0:2 * F].rearrange("p r (k f) -> p r k f", f=F)).then_inc(b1_ready, 1)

            def split_second(g, u):
                act.wait_ge(rest_ready, g + 1)
                act.copy(stage_b[0:PB, u, :, 2 * F:3 * F], rest_b[0:PB, u % 2, :, :]).then_inc(b2_ready, 1)

            def table_b(g, u):
                known = isinstance(g, int)
                if not known or g < NG:
                    split_first(g, u)
                if not known or g >= 1:
                    split_second(g - 1, (u - 1) % STAGES)

            steps(act, 0, NG + 1, STAGES, STAGES, table_b, tail=1)
            act.wait_ge(tab_ready, 2 * NG)
            act.wait_ge(ld_w, 16 * N_LD_W)

            def evacuate_ea(q, u):
                act.wait_ge(ea_t, q + 1)
                if reached(q, 2):
                    act.wait_ge(z_mm, q - 1)
                act.copy(eaT[:, u % 2, :], ps_eaT[:, 0:PAIR]).then_inc(ea_e, 1)

            def softplus_exp(q, u):
                act.wait_ge(z_mm, q + 1)
                if reached(q, 2):
                    act.wait_ge(z_ln, q - 1)
                act.activation(ex[:, u % 2, 0:QUAD], ps[:, 2 * (u % 2), :], ACT.Exp)
                act.activation(ex[:, u % 2, QUAD:QUAD + PAIR], ps[:, 2 * (u % 2) + 1, 0:PAIR], ACT.Exp,
                               bias=be1c[:, 0:1]).then_inc(z_exp, 1)

            def softplus_ln(q, u):
                act.wait_ge(z_clamp, q + 1)
                if reached(q, 2):
                    act.wait_ge(hid_b, q - 1)
                act.activation(lg[:, u % 2, :], ex[:, u % 2, :], ACT.Ln, bias=halfc[:, 0:1], scale=0.5).then_inc(z_ln, 1)

            def evacuate(q, u):
                evacuate_ea(q, u)
                act.wait_ge(oh_t, q + 1)
                act.copy(ohT[:, u % 2, :], ps_ohT[:, :]).then_inc(oh_e, 1)

            def fast_step(q, u):
                if isinstance(q, int) and q == 0:
                    evacuate(0, 0)
                softplus_exp(q, u)
                if not isinstance(q, int) or q + 1 < NQ:
                    evacuate(q + 1, (u + 1) % RING)
                softplus_ln(q, u)

            def general_step(q, u):
                evacuate_ea(q, u)
                softplus_exp(q, u)
                softplus_ln(q, u)

            general = general_of(act)
            with act.If(general):
                steps(act, 0, NQ, RING, RING, general_step, tail=1)
            with act.Else():
                steps(act, 0, NQ, RING, RING, fast_step, tail=1)

            def node_exp(k, u):
                act.wait_ge(n_clamp, k + 1)
                act.activation(ex[:, u, 0:2 * PB], ex[:, u, 0:2 * PB], ACT.Exp).then_inc(n_exp, 1)

            def node_ln(k, u):
                act.wait_ge(n_exp, k + 1)
                if reached(k, 2):
                    act.wait_ge(n_hid, k - 1)
                act.activation(lg[:, u, 0:2 * PB], ex[:, u, 0:2 * PB], ACT.Ln, bias=halfc[:, 0:1],
                               scale=0.5).then_inc(n_ln, 1)

            def node_square(k, u):
                act.wait_ge(y_add, k + 1)
                if reached(k, 2):
                    act.wait_ge(y_sum, k - 1)
                act.activation(sq[0:PB, u, :, :], dd[0:PB, u, :, :], ACT.Square).then_inc(y_sq, 1)

            def node_ln_variance(k, u):
                act.wait_ge(y_sum, k + 1)
                act.activation(lvar[0:PB, u, :], ssum[0:PB, u, :], ACT.Ln, bias=epsc[0:PB, 0:1],
                               scale=1.0 / D).then_inc(y_lv, 1)

            def node_rstd(k, u):
                act.wait_ge(y_lv, k + 1)
                act.activation(rstd[0:PB, u, :], lvar[0:PB, u, :], ACT.Exp, scale=-0.5).then_inc(y_rstd, 1)

            def node_step(k, u):
                known = isinstance(k, int)
                if not known or k < NG:
                    node_exp(k, u)
                if not known or k >= 2:
                    node_ln_variance(k - 2, u)
                if not known or k < NG:
                    node_ln(k, u)
                if not known or k >= 2:
                    node_rstd(k - 2, u)
                if not known or 1 <= k <= NG:
                    node_square(k - 1, 1 - u)

            steps(act, 0, NG + 2, 4, 2, node_step, tail=2)

        @block.vector
        def _(dve):
            chain = [0]

            def link(ins):
                chain[0] += 1
                ins.then_inc(dve_chain, 1)
                dve.wait_ge(dve_chain, chain[0])

            dve.memset(we1[:, :], 0.0)
            dve.memset(we2[:, :], 0.0)
            dve.memset(brow[:, :, :, :], 0.0)
            dve.memset(biasb[:, :], 0.0)
            dve.memset(ones_b[:, :], 1.0)
            dve.memset(cexp[:, :], -17.5)
            dve.memset(epsc[:, :], EPS)
            dve.memset(halfc[:, :], 0.5)
            dve.memset(stage_b[:, :, :, 3 * F:4 * F], 0.0).then_inc(zeroed, 1)

            dve.wait_ge(ld_wn, 16 * 4)
            link(dve.tensor_reduce(bmean[:, :], bs2r[:, :], AX_X, ALU.add))
            link(dve.tensor_scalar(bmean[:, :], bmean[:, :], 1.0 / D, None, ALU.mult))
            link(dve.tensor_scalar(bs2r[:, :], bs2r[:, :], bmean[:, 0:1], None, ALU.subtract))

            def table_a(g, u):
                dve.wait_ge(tab_mm, g + 1)
                if reached(g, STAGES):
                    dve.wait_ge(a_stored[u], per_ring(g, u, STAGES, 16) - 16)
                dve.tensor_tensor(stage_a[0:PB, u, :, :].rearrange("p (k r) f -> p r k f", r=2),
                                  ps[0:PB, 2 * (u % 2):2 * (u % 2) + 2, 0:2 * F].rearrange("p r (k f) -> p r k f", f=F),
                                  bn1r[0:PB, :].unsqueeze(1).unsqueeze(1).broadcast_to([PB, 2, 2, F]),
                                  ALU.add).then_inc(tab_ready, 1)
                dve.tensor_reduce(xmean[0:PB, bass.ds(g * 4, 4)], xs[0:PB, bass.ds(g * 4, 4), :], AX_X,
                                  ALU.add).then_inc(x_sum, 1)
                dve.wait_ge(x_sum, g + 1)
                dve.scalar_tensor_tensor(out=xs[0:PB, bass.ds(g * 4, 4), :], in0=xs[0:PB, bass.ds(g * 4, 4), :],
                                         scalar=2.0, in1=bs2r[0:PB, :].unsqueeze(1).broadcast_to([PB, 4, D]),
                                         op0=ALU.mult, op1=ALU.add)

            steps(dve, 0, G1, G1, STAGES, table_a)
            dve.wait_ge(ld_src, 16 * N_LD_ROWS)
            if RG > 1:
                dve.tensor_copy(rows_f[:, 0, 0:RG - 1, :], rows_i[:, 0, 0:RG - 1, :])
            dve.tensor_copy(rows_f[0:RL, 0, RG - 1, :], rows_i[0:RL, 0, RG - 1, :]).then_inc(rows_ready[0], 1)
            for g in range(RG):
                rows = P if g < RG - 1 else RL
                dve.wait_ge(row_t, g + 1)
                tv = srcT[:, 2 * P * g:2 * (P * g + rows)].rearrange("p (r j) -> p j r", j=2)
                pv = ps[:, 6 + g % 2, 0:PAIR].rearrange("p (j r) -> p j r", j=2)[:, :, 0:rows]
                dve.tensor_copy(tv, pv).then_inc(row_dve, 1)

            dve.wait_ge(rows_ready[1], 1)
            if RG > 1:
                dve.tensor_reduce(dmin[:, 0:RG - 1], rows_f[:, 1, 0:RG - 1, :], AX_X, ALU.min)
            link(dve.tensor_reduce(dmin[0:RL, RG - 1:RG], rows_f[0:RL, 1, RG - 1, :], AX_X, ALU.min))
            if RG > 1:
                dve.tensor_scalar(w_i[:, 0:RG - 1], dmin[:, 0:RG - 1], float(N - W), None, ALU.min)
            dve.tensor_scalar(w_i[0:RL, RG - 1:RG], dmin[0:RL, RG - 1:RG], float(N - W), None, ALU.min).then_inc(w_ready, 1)

            steps(dve, G1, G2, 0, STAGES, table_a)

            dve.wait_ge(row_act, RG)
            dve.wait_ge(w_loaded, 16)
            link(dve.tensor_tensor(relT[:, :].rearrange("p (r j) -> p r j", j=2),
                                   dstT[:, :].rearrange("p (r j) -> p r j", j=2),
                                   w_all[:, :].unsqueeze(2).broadcast_to([P, NPAIR, 2]), ALU.subtract))
            dve.tensor_reduce(relmax[:, :], relT[:, :], AX_X, ALU.max).then_inc(relm_ready, 1)

            dve.wait_ge(ld_bd, 16 * 10)
            dve.wait_ge(ld_w, 16 * N_LD_W)
            bflat = brow[:, :, :, :].rearrange("p h k d -> p (h k d)")
            dve.tensor_scalar(be1l[:, :], be1c[:, :], LN2, None, ALU.subtract)
            dve.tensor_scalar(bs1l[:, :], bs1c[:, :], LN2, None, ALU.subtract)
            link(dve.tensor_copy(brow1[:, :], bflat))
            link(dve.tensor_tensor(bflat, bflat, brow1[:, :], ALU.subtract))
            link(dve.tensor_copy(brow2[:, :], bflat))
            link(dve.tensor_tensor(bflat, bflat, brow2[:, :], ALU.subtract))
            dve.tensor_copy(biasb[0:1, :], brow1[0:1, :])
            dve.tensor_copy(biasb[32:33, :], brow2[32:33, :])
            dve.tensor_copy(biasb[64:65, :], bflat[64:65, :])
            link(dve.tensor_reduce(ws2m[:, :], ws2[:, :], AX_X, ALU.add))
            link(dve.tensor_scalar(ws2m[:, :], ws2m[:, :], 1.0 / D, None, ALU.mult))
            dve.tensor_scalar(ws2[:, :], ws2[:, :], ws2m[:, 0:1], None, ALU.subtract)
            dve.wait_ge(consts, 2)
            dve.tensor_copy(identb[:, :], ident[:, :])
            dve.wait_ge(iotas, 1)
            for h in range(2):
                dve.tensor_copy(iota_w[:, h * W:(h + 1) * W], iota_i[:, 0:W])
            steps(dve, G2, NG, 0, STAGES, table_a)
            dve.wait_ge(relm_t, 1)
            link(dve.tensor_reduce(flagf[0:1, 0:1], ps[0:1, 6, 0:P], AX_X, ALU.max))
            dve.tensor_scalar(flag_i[0:1, 0:1], flagf[0:1, 0:1], W - 0.5, None, ALU.is_gt).then_inc(flag_ready, 1)
            dve.wait_ge(cut_exp, 1)
            link(dve.tensor_scalar(cutT[:, :], cutT[:, :], 1.0, None, ALU.add))
            link(dve.reciprocal(cutT[:, :], cutT[:, :]))
            for p0, p1 in ((REM // 2, 64), (64, P)):
                if p0 < p1:
                    link(dve.memset(cutT[p0:p1, NT - 2:NT], 0.0))
            def rest_of_b(g, u):
                dve.wait_ge(b1_ready, g + 1)
                if reached(g, 2):
                    dve.wait_ge(tab_ready, g + (NG - 1))
                dve.tensor_tensor(rest_b[0:PB, u % 2, :, :].rearrange("p (k r) f -> p r k f", r=2),
                                  ps[0:PB, 2 * u:2 * u + 2, 0:2 * F].rearrange("p r (k f) -> p r k f", f=F),
                                  stage_b[0:PB, u, :, 0:F].rearrange("p (k r) f -> p r k f", r=2),
                                  ALU.subtract).then_inc(rest_ready, 1)

            def third_of_b(g, u):
                dve.wait_ge(b2_ready, g + 1)
                dve.tensor_tensor(stage_b[0:PB, u, :, F:2 * F], rest_b[0:PB, u % 2, :, :],
                                  stage_b[0:PB, u, :, 2 * F:3 * F], ALU.subtract).then_inc(tab_ready, 1)

            def table_b(g, u):
                known = isinstance(g, int)
                if not known or g < NG:
                    rest_of_b(g, u)
                if not known or g >= 1:
                    third_of_b(g - 1, (u - 1) % STAGES)
                if not known or g < NG:
                    ins = dve.scalar_tensor_tensor(
                        out=xs[0:PB, bass.ds(g * 4, 4), :], in0=xmean[0:PB, bass.ds(g * 4, 4)].unsqueeze(2).broadcast_to([PB, 4, D]),
                        scalar=-2.0 / D, in1=xs[0:PB, bass.ds(g * 4, 4), :], op0=ALU.mult, op1=ALU.add)
                    ins.then_inc(xc_ready, 1)

            steps(dve, 0, NG + 1, STAGES, STAGES, table_b, tail=1)
            for k in range(STAGES):
                dve.wait_ge(a_stored[k], 16 * uses(k, STAGES))
                dve.wait_ge(b_stored[k], 16 * uses(k, STAGES))

            def one_hot(q, u):
                if reached(q, RING):
                    dve.wait_ge(sc_mm, q - (RING - 1))
                dve.tensor_tensor(oh[:, u, :, :], iota_w[:, :].unsqueeze(1).broadcast_to([P, 4, P]),
                                  relT[:, quad_cols(q, 4, 4)].unsqueeze(2).broadcast_to([P, 4, P]),
                                  ALU.is_equal).then_inc(oh_b, 1)

            def clamp(q, u):
                dve.wait_ge(z_exp, q + 1)
                dve.tensor_scalar(ex[:, u % 2, :], ex[:, u % 2, :], CLAMP, None, ALU.min).then_inc(z_clamp, 1)

            def hidden(q, u):
                dve.wait_ge(z_ln, q + 1)
                if reached(q, 2):
                    dve.wait_ge(hg_mm, q - 1)
                dve.scalar_tensor_tensor(out=hid[:, u % 2, 0:QUAD], in0=ps[:, 2 * (u % 2), :], scalar=LN2,
                                         in1=lg[:, u % 2, 0:QUAD], op0=ALU.subtract, op1=ALU.max)
                dve.scalar_tensor_tensor(out=hid[:, u % 2, QUAD:QUAD + PAIR], in0=ps[:, 2 * (u % 2) + 1, 0:PAIR],
                                         scalar=be1l[:, 0:1], in1=lg[:, u % 2, QUAD:QUAD + PAIR],
                                         op0=ALU.add, op1=ALU.max).then_inc(hid_b, 1)

            def message(q, u, scattered=sc_mm):
                dve.wait_ge(hg_mm, q + 1)
                dve.tensor_tensor(gcut[:, :].rearrange("p (t d) -> p t d", d=D),
                                  ps_hg[:, PAIR:2 * PAIR].rearrange("p (t d) -> p t d", d=D),
                                  cutT[:, quad_cols(q, 4, 4)].unsqueeze(2).broadcast_to([P, 4, D]),
                                  ALU.mult).then_inc(gc_b, 1)
                dve.wait_ge(gc_b, q + 1)
                if scattered is not None:
                    if reached(q, 2):
                        dve.wait_ge(scattered, q - 1)
                dve.tensor_tensor(msg[:, u % 2, :, :].rearrange("p t d -> p (t d)"), ps_hg[:, 0:PAIR],
                                  gcut[:, :], ALU.mult).then_inc(msg_b, 1)

            firsts = [None] * 4

            def load_firsts(q):
                _, firsts[:] = nc.values_load_multi_w_load_instructions(
                    w_all[0:1, bass.ds(q * 2, 4)], engines=(mybir.EngineType.DVE,), min_val=0, max_val=N - W)

            def flush(q, u):
                dve.wait_ge(sc_mm, q + 1)
                if reached(q, 1):
                    dve.wait_ge(flushed, q)
                for k in range(2):
                    w = firsts[2 * (u % 2) + k]
                    half = slice(k * D, (k + 1) * D)
                    ins = dve.tensor_tensor(acc[half, bass.ds(w, W)], acc[half, bass.ds(w, W)],
                                            ps_s[half, 0:W], ALU.add)
                ins.then_inc(flushed, 1)

            def fast_step(s, u):
                known = isinstance(s, int)
                if known and s == 0:
                    one_hot(0, 0)
                    one_hot(1, 1)
                if u % 2 == 0 and (not known or 2 <= s <= NQ):
                    load_firsts(s - 2)
                if known and s == NQ + 1 and NQ % 2 == 1:
                    firsts[0:2] = [dve.value_load(w_all[0:1, NPAIR - 2 + k:NPAIR - 1 + k], min_val=0, max_val=N - W)
                                   for k in range(2)]
                if not known or s < NQ:
                    clamp(s, u)
                if not known or s + 2 < NQ:
                    one_hot(s + 2, (u + 2) % RING)
                if not known or s >= 2:
                    flush(s - 2, (u - 2) % RING)
                if not known or 1 <= s <= NQ:
                    message(s - 1, (u - 1) % RING)
                if not known or s < NQ:
                    hidden(s, u)

            def general_step(q, u):
                clamp(q, u)
                hidden(q, u)
                message(q, u, None)
                link2 = q * (SB // 2)
                dve.tensor_copy(gen_rel[:, 0, :], dstT[:, quad_cols(q, 4, 4)]).then_inc(g_rel, 1)
                with dve.Fori(0, SB // 2) as b:
                    for k in range(2):
                        done = q * SB + b * 2 + k + 2 + q
                        dve.wait_ge(g_rel, done)
                        dve.tensor_tensor(gen_oh[:, k, :, :], iota_n[:, :].unsqueeze(1).broadcast_to([P, 4, P]),
                                          gen_rel[:, k, :].unsqueeze(2).broadcast_to([P, 4, P]),
                                          ALU.is_equal).then_inc(g_oh[k], 1)
                        dve.tensor_scalar(gen_rel[:, 1 - k, :], gen_rel[:, k, :], float(P), None,
                                          ALU.subtract).then_inc(g_rel, 1)
                        dve.wait_ge(g_mm[k], link2 + b + 1)
                        dve.wait_ge(g_add[1 - k], link2 + b + 1)
                        cols = bass.ds((b * 2 + k) * P, P)
                        dve.tensor_tensor(acc[0:D, cols], acc[0:D, cols], ps_s[0:D, 0:P],
                                          ALU.add).then_inc(g_add[k], 1)
                dve.memset(flagf[0:1, 1:2], 0.0).then_inc(flushed, 1)

            dve.wait_ge(acc_zeroed, 1)
            general = general_of(dve)
            with dve.If(general):
                dve.tensor_copy(relT[:, :].bitcast(I32), dstT[:, :]).then_inc(g_rel, 1)
                dve.memset(flagf[0:1, 1:2], 0.0).then_inc(g_add[1], 1)
                steps(dve, 0, NQ, RING, RING, general_step, tail=1)
            with dve.Else():
                steps(dve, 0, NQ + 2, RING, RING, fast_step, tail=4)

            def node_clamp(k, u):
                dve.wait_ge(n_mm, k + 1)
                if reached(k, 2):
                    dve.wait_ge(n_ln, k - 1)
                dve.tensor_scalar(ex[:, u, 0:2 * PB], ps[:, u, 0:2 * PB], bs1c[:, 0:1], ZMAX, ALU.add,
                                  ALU.min).then_inc(n_clamp, 1)

            def node_max(k, u):
                dve.wait_ge(n_ln, k + 1)
                if reached(k, 2):
                    dve.wait_ge(y_mm, k - 1)
                dve.scalar_tensor_tensor(out=hid[:, u, 0:2 * PB], in0=ps[:, u, 0:2 * PB], scalar=bs1l[:, 0:1],
                                         in1=lg[:, u, 0:2 * PB], op0=ALU.add, op1=ALU.max).then_inc(n_hid, 1)

            def node_add(k, u):
                dve.wait_ge(y_mm, k + 1)
                if reached(k, 2):
                    dve.wait_ge(y_out, k - 1)
                dve.tensor_tensor(dd[0:PB, u, :, :].rearrange("p (h c) d -> p h (c d)", h=2),
                                  ps[0:PB, 4 + 2 * u:6 + 2 * u, 0:2 * D],
                                  xs[0:PB, bass.ds(k * 4, 4), :].rearrange("p (h c) d -> p h (c d)", h=2),
                                  ALU.add).then_inc(y_add, 1)

            def node_sum(k, u):
                dve.wait_ge(y_sq, k + 1)
                dve.tensor_reduce(ssum[0:PB, u, :], sq[0:PB, u, :, :], AX_X, ALU.add).then_inc(y_sum, 1)

            def node_scale(k, u):
                dve.wait_ge(y_rstd, k + 1)
                if reached(k, 2):
                    dve.wait_ge(s_out[u], per_ring(k, u, 2, 16) - 16)
                dve.tensor_tensor(outs[0:PB, u, :, :], dd[0:PB, u, :, :],
                                  rstd[0:PB, u, :].unsqueeze(2).broadcast_to([PB, 4, D]),
                                  ALU.mult).then_inc(y_out, 1)

            def node_step(k, u):
                known = isinstance(k, int)
                if not known or k < NG:
                    node_clamp(k, u)
                if not known or k >= 2:
                    node_sum(k - 2, u)
                if not known or 1 <= k <= NG:
                    node_add(k - 1, 1 - u)
                if not known or k < NG:
                    node_max(k, u)
                if not known or k >= 2:
                    node_scale(k - 2, u)

            steps(dve, 0, NG + 2, 4, 2, node_step, tail=2)


_INS = ["x", "src", "dst", "edge_attr_64", "edge_weight1"] + [
    "L0_gnn_" + n for n in ("We1", "be1", "We2", "be2", "Wn1", "bn1", "Wn2", "bn2", "Ws1", "bs1", "Ws2", "bs2")]


def kernel(**inputs):
    import numpy as _np
    import concourse.bacc as _bacc
    from concourse import mybir as _mybir
    from concourse.bass_utils import run_bass_kernel_spmd as _run

    nc = _bacc.Bacc("TRN2", target_bir_lowering=False, num_devices=1)
    arrays, args = {}, []
    for name in _INS:
        a = _np.ascontiguousarray(inputs[name])
        arrays[f"in_{name}_dram"] = a
        args.append(nc.dram_tensor(f"in_{name}_dram", a.shape, _mybir.dt.from_np(a.dtype), kind="ExternalInput").ap())
    n, d = inputs["x"].shape
    out = nc.dram_tensor("out_0_dram", (n, d), _mybir.dt.float32, kind="ExternalOutput").ap()
    gnn_layer(nc, *args, out)
    r = _run(nc, [arrays], core_ids=[0])
    return r.results[0]["out_0_dram"]
```
